# Optimizing a Trainium2 kernel written in Bass

```python
import numpy as np
import jax
import jax.numpy as jnp

def _softmax(x, axis=-1):
    return jax.nn.softmax(x, axis=axis)

def _gelu(x):
    return jax.nn.gelu(x, approximate=True)

def _silu(x):
    return jax.nn.silu(x)

def _sigmoid(x):
    return jax.nn.sigmoid(x)

def _layernorm(x, axis=-1, eps=1e-05):
    m = jnp.mean(x, axis=axis, keepdims=True)
    v = jnp.var(x, axis=axis, keepdims=True)
    return (x - m) / jnp.sqrt(v + eps)

def _scatter_add(tgt, idx, src, axis=0):
    return tgt.at[idx].add(src)

def _segment_sum(src, seg, n):
    return jax.ops.segment_sum(src, seg, n)
kernel_name = 'mk_adj_ffn_d1_adj_r2_360ab9'

def setup_inputs(seed: int=0):
    np.random.seed(seed)
    _w = jnp.asarray

    def _rec_inputs():
        import jax
        import jax.numpy as jnp
        _gk = jax.random.key(seed)
        x = -0.0002928 + 1 * jax.random.normal(jax.random.fold_in(_gk, 1), (128, 128, 128), jnp.float32)
        _a = jax.random.bernoulli(jax.random.fold_in(_gk, 2), 0.125, (128, 128, 128))
        _a = jnp.logical_or(_a, jnp.swapaxes(_a, -1, -2))
        _a = jnp.logical_or(_a, jnp.eye(128, dtype=bool))
        _af = _a.astype(jnp.float32)
        _af = _af * jax.random.uniform(jax.random.fold_in(_gk, 3), (128, 128, 128), jnp.float32, 0.05, 1)
        adj = _af
        return (x, adj)
    x, adj = _rec_inputs()

    def _L0_gnn_setup():
        import jax, jax.numpy as jnp
        import numpy as np
        B, N, F_IN, F_OUT = (8, 1024, 128, 128)
        key = jax.random.key(seed)
        k1, k2, k3, k4 = jax.random.split(key, 4)
        node_features = jax.random.normal(k1, (B, N, F_IN), dtype=jnp.float32)
        adj_matrix = jax.random.uniform(k2, (B, N, N), dtype=jnp.float32)
        lim = 1.0 / np.sqrt(F_IN)
        W = jax.random.uniform(k3, (F_OUT, F_IN), minval=-lim, maxval=lim, dtype=jnp.float32)
        b = jax.random.uniform(k4, (F_OUT,), minval=-lim, maxval=lim, dtype=jnp.float32)
        return {'node_features': node_features, 'adj_matrix': adj_matrix, 'W': W, 'b': b}
    _L0_gnn_all = _L0_gnn_setup()
    _L0_gnn_in = {k: v for k, v in _L0_gnn_all.items() if k in ('W', 'b')}
    del _L0_gnn_all

    def _L0_ffn_setup():
        import jax, jax.numpy as jnp
        import numpy as np
        C = 128
        HID = 512
        E = 8
        TEMP = 1.0
        key = jax.random.key(seed)
        ks = jax.random.split(key, 7)
        x = jax.random.normal(ks[0], (8, 8192, C), dtype=jnp.float32)
        W1 = jax.random.normal(ks[1], (C, HID), dtype=jnp.float32) * 0.02
        b1 = jnp.zeros((HID,), dtype=jnp.float32)
        Wg = jax.random.normal(ks[2], (HID, E), dtype=jnp.float32) * 0.02
        bg = jnp.zeros((E,), dtype=jnp.float32)
        Wd = jax.random.normal(ks[3], (E, HID, C), dtype=jnp.float32) * 0.02
        bd = jnp.zeros((E, C), dtype=jnp.float32)
        return {'x': x, 'W1': W1, 'b1': b1, 'Wg': Wg, 'bg': bg, 'Wd': Wd, 'bd': bd}
    _L0_ffn_all = _L0_ffn_setup()
    _L0_ffn_in = {k: v for k, v in _L0_ffn_all.items() if k in ('W1', 'b1', 'Wg', 'bg', 'Wd', 'bd')}
    del _L0_ffn_all
    return {'x': x, 'adj': adj, 'L0_gnn_W': _L0_gnn_in['W'], 'L0_gnn_b': _L0_gnn_in['b'], 'L0_ffn_W1': _L0_ffn_in['W1'], 'L0_ffn_b1': _L0_ffn_in['b1'], 'L0_ffn_Wg': _L0_ffn_in['Wg'], 'L0_ffn_bg': _L0_ffn_in['bg'], 'L0_ffn_Wd': _L0_ffn_in['Wd'], 'L0_ffn_bd': _L0_ffn_in['bd']}

def reference(x, adj, L0_gnn_W, L0_gnn_b, L0_ffn_W1, L0_ffn_b1, L0_ffn_Wg, L0_ffn_bg, L0_ffn_Wd, L0_ffn_bd):
    import jax
    import jax.numpy as jnp

    def _L0_gnn_ref(node_features, adj_matrix, W, b):
        import jax, jax.numpy as jnp
        import numpy as np
        B, N, F_IN, F_OUT = (8, 1024, 128, 128)
        degree = jnp.sum(adj_matrix, axis=-1)
        d_inv_sqrt = jnp.power(degree, -0.5)
        d_inv_sqrt = jnp.where(jnp.isinf(d_inv_sqrt), 0.0, d_inv_sqrt)
        norm_adj = adj_matrix * d_inv_sqrt[:, :, None] * d_inv_sqrt[:, None, :]
        transformed = jnp.einsum('bnf,of->bno', node_features, W) + b
        output = jnp.einsum('bnm,bmo->bno', norm_adj, transformed)
        return jax.nn.relu(output)

    def _L0_ffn_ref(x, W1, b1, Wg, bg, Wd, bd):
        import jax, jax.numpy as jnp
        import numpy as np
        C = 128
        HID = 512
        E = 8
        TEMP = 1.0
        orig_shape = x.shape
        xf = x.reshape(-1, orig_shape[-1])
        H = jax.nn.gelu(xf @ W1 + b1, approximate=False)
        probs = jax.nn.softmax((H @ Wg + bg) / TEMP, axis=-1)
        assign = jnp.argmax(probs, axis=-1)
        out = jnp.zeros_like(xf)
        for e in range(Wd.shape[0]):
            y = H @ Wd[e] + bd[e]
            sel = (assign == e)[:, None]
            out = out + jnp.where(sel, probs[:, e:e + 1] * y, 0.0)
        return out.reshape(orig_shape)
    x = x + _L0_gnn_ref(_layernorm(x, axis=-1), adj, L0_gnn_W, L0_gnn_b)
    x = x + _L0_ffn_ref(_layernorm(x, axis=-1), L0_ffn_W1, L0_ffn_b1, L0_ffn_Wg, L0_ffn_bg, L0_ffn_Wd, L0_ffn_bd)
    return x

_drawn_inputs = setup_inputs


def setup_inputs(seed=0):
    import zlib

    import numpy as np

    out = dict(_drawn_inputs(seed))
    spreads = {'L0_ffn_b1': (0.0, 0.8), 'L0_ffn_bg': (0.0, 0.432), 'L0_ffn_bd': (0.0, 0.587)}
    factors = {'L0_ffn_W1': 5.062, 'L0_ffn_Wg': 4.886, 'L0_ffn_Wd': 6.693}
    for name, (base, spread) in spreads.items():
        noise = np.random.default_rng([zlib.crc32(name.encode()), seed]).standard_normal(out[name].shape)
        drawn = base * np.exp(spread * noise) if base else spread * noise
        out[name] = jnp.asarray(drawn.astype(out[name].dtype))
    for name, factor in factors.items():
        out[name] = (out[name] * factor).astype(out[name].dtype)
    return out
```

```python
from contextlib import ExitStack

import concourse.bass as bass
from concourse import mybir

ALU = mybir.AluOpType
ACT = mybir.ActivationFunctionType
AX_X = mybir.AxisListType.X
F32 = mybir.dt.float32
F32R = mybir.dt.float32r
BF16 = mybir.dt.bfloat16
I32 = mybir.dt.int32

P = 128
GRAPHS = 128
TOKENS = GRAPHS * P
D = 128
HID = 512
HC = HID // P
E = 8
T = 4
GROUPS = GRAPHS // T
GT = T * P
EPS = 1e-5
ROW = D + 4
C_NMR, C_RSTD, C_PROB, C_TOK = D, D + 1, D + 2, D + 3
REGION = TOKENS + P
TILES = TOKENS // P + E
QUADS = TILES // T
SLOTS = 4


class Step:

    def __init__(self, k, c):
        self.n = 4 * k + c
        self.slot4, self.slot2 = c % 4, c % 2
        self.nth4, self.nth2 = k + c // 4, 2 * k + c // 2
        self.uses_back2 = k + (c + 2) // 4
        self.fixed = isinstance(k, int)


def moe_gnn_kernel(nc, x, adj, gnn_w, gnn_b, w1, b1, wg, bg, wd, bd, out):
    with ExitStack() as ctx:
        def sb(name, shape, dt=F32):
            return ctx.enter_context(nc.sbuf_tensor(name, shape, dt))

        def bank(name, shape=(P, 512), dt=F32):
            return ctx.enter_context(nc.psum_tensor(name, list(shape), dt))

        def sem(name):
            return ctx.enter_context(nc.semaphore(name))

        table = nc.dram_tensor("table", [E * REGION + P, ROW], F32).ap()

        ident = sb("ident", [P, P])
        earlier = sb("earlier", [P, P], BF16)
        ones = sb("ones", [P, P], BF16)
        gate_sum = sb("gate_sum", [P, E])
        first_wins = sb("first_wins", [P, T, E])
        seed_tok = sb("seed_tok", [P, T], I32)
        tok_f = sb("tok_f", [P, T])
        minus_half = sb("minus_half", [P, 2 * T])
        gnn_w_sb = sb("gnn_w_sb", [P, D])
        gnn_wt = sb("gnn_wt", [P, D])
        gnn_b_all = sb("gnn_b_all", [P, T, D])
        w1_sb = sb("w1_sb", [P, HID])
        w1_hi = sb("w1_hi", [P, HID], F32R)
        w1_lo = sb("w1_lo", [P, HID], F32R)
        b1_col = sb("b1_col", [P, HC])
        wg_sb = sb("wg_sb", [P, HC, 32])
        wg_in = sb("wg_in", [P, HC, E])
        bg_col = sb("bg_col", [P, 1])
        wd_sb = sb("wd_sb", [P, HC, E * D])
        bd_row = sb("bd_row", [1, E * D])
        bd_rest = sb("bd_rest", [1, E * D])
        bd_part = sb("bd_part", [1, 3, E * D], BF16)
        bd3 = sb("bd3", [3, E * D], BF16)

        x_in = sb("x_in", [P, 2, T, D])
        adj_in = sb("adj_in", [P, 2, T, P])
        bn1 = sb("bn1", [P, T, 6])
        mean1 = sb("mean1", [P, T])
        m_sum = sb("m_sum", [P, T])
        m_diff = sb("m_diff", [P, T])
        m_sq = sb("m_sq", [P, T])
        m_between = sb("m_between", [P, T])
        m_within = sb("m_within", [P, T])
        pace = sb("pace", [1, 1])
        pace_out = sb("pace_out", [1, SLOTS])
        deg = sb("deg", [P, T])
        pow_in = sb("pow_in", [P, 2 * T])
        pow_out = sb("pow_out", [P, 2 * T])
        dinv = sb("dinv", [P, 2, T])
        xhat = sb("xhat", [P, 2, T, D])
        xhat_t = sb("xhat_t", [P, GT])
        adj_t = sb("adj_t", [P, T, P])
        feats = sb("feats", [P, T, D])
        agg = sb("agg", [P, T, D])
        rows = sb("rows", [P, SLOTS, T, ROW])
        bn2 = sb("bn2", [P, T, 6])
        mean2 = sb("mean2", [P, T])
        var2 = sb("var2", [P, T])
        x2hat = sb("x2hat", [P, T, D])
        x2hat_t = sb("x2hat_t", [P, 2, GT])
        hidden = sb("hidden", [P, 2, HC, GT])
        logits_t = sb("logits_t", [P, GT])
        top = sb("top", [P, T])
        below = sb("below", [P, T, E])
        cand = sb("cand", [P, T, E])
        best = sb("best", [P, T])
        chosen = sb("chosen", [P, T, E], BF16)
        tanh_half = sb("tanh_half", [P, T, E])
        soft = sb("soft", [P, T, E])
        soft_r = sb("soft_r", [P, T, E])
        soft_sum = sb("soft_sum", [P, T])
        denom = sb("denom", [P, T])
        base = sb("base", [P, E])
        place = sb("place", [P, T, E])
        place_own = sb("place_own", [P, T, E])
        place_sum = sb("place_sum", [P, T])
        index = sb("index", [P, 2, T], I32)

        region_i = sb("region_i", [P, E], I32)
        region0 = sb("region0", [P, E])
        count_f = sb("count_f", [1, E])
        count_i = sb("count_i", [1, E], I32)
        ntile_i = sb("ntile_i", [1, E], I32)
        ntile_f = sb("ntile_f", [1, E])
        upto = sb("upto", [1, E, E])
        ntile_upto = sb("ntile_upto", [1, E, E])
        last_tile = sb("last_tile", [1, E])
        jump = sb("jump", [1, E])
        tile_no_i = sb("tile_no_i", [1, TILES], I32)
        tile_no = sb("tile_no", [1, TILES])
        passed = sb("passed", [1, TILES, E])
        jumped = sb("jumped", [1, TILES, E])
        tile_e = sb("tile_e", [1, TILES])
        tile_r = sb("tile_r", [1, TILES])
        tile_r2 = sb("tile_r2", [1, TILES])
        tile_col = sb("tile_col", [1, TILES], I32)
        tile_row = sb("tile_row", [1, TILES], I32)
        fill_row = sb("fill_row", [1, E], I32)
        filler = sb("filler", [P, ROW])

        rows_b = sb("rows_b", [P, SLOTS, T, ROW])
        yhat = sb("yhat", [P, T, D])
        yhat_hi = sb("yhat_hi", [P, 2, GT], F32R)
        yhat_lo = sb("yhat_lo", [P, 2, GT], F32R)
        result = sb("result", [P, 2, T, D])

        ps_x = bank("ps_x")
        ps_a = bank("ps_a")
        ps_f = bank("ps_f")
        ps_u = bank("ps_u")
        ps_h = [bank("ps_h0"), bank("ps_h1")]
        ps_g = bank("ps_g")
        ps_r = bank("ps_r")
        logit_ps = ps_r[:, 0:T * E].rearrange("p (t e) -> p t e", t=T)
        rank_ps = ps_r[:, 64:64 + (T + 1) * E].rearrange("p (t e) -> p t e", t=T + 1)
        ps_y = [ps_a, ps_f, ps_u, ps_g]

        w_in = sem("w_in")
        const_pool = sem("const_pool")
        const_dve = sem("const_dve")
        wt_ps = sem("wt_ps")
        wt_sb = sem("wt_sb")
        bd_in = sem("bd_in")
        v1_setup = sem("v1_setup")
        x_load = [sem(f"x_load{s}") for s in range(2)]
        a_load = [sem(f"a_load{s}") for s in range(2)]
        v1_step = sem("v1_step")
        stat1 = sem("stat1")
        pow1 = sem("pow1")
        dinv_ok = sem("dinv_ok")
        xhat_ok = sem("xhat_ok")
        xt_ps = sem("xt_ps")
        xt_sb = sem("xt_sb")
        at_ps = sem("at_ps")
        at_sb = sem("at_sb")
        f_ps = sem("f_ps")
        f_sb = sem("f_sb")
        u_ps = sem("u_ps")
        agg_ok = sem("agg_ok")
        x1_ok = sem("x1_ok")
        v4_step = sem("v4_step")
        stat2 = sem("stat2")
        pow2 = sem("pow2")
        v5_step = sem("v5_step")
        x2hat_ok = sem("x2hat_ok")
        x2t_ps = sem("x2t_ps")
        x2t_sb = sem("x2t_sb")
        h_ps = sem("h_ps")
        h_sb = sem("h_sb")
        g_ps = sem("g_ps")
        lt_sb = sem("lt_sb")
        l_ps = sem("l_ps")
        v6_step = sem("v6_step")
        chosen_ok = sem("chosen_ok")
        tanh_ok = sem("tanh_ok")
        rank_ok = sem("rank_ok")
        v7_step = sem("v7_step")
        paced = sem("paced")
        row_ok = sem("row_ok")
        scattered = [sem(f"scattered{s}") for s in range(SLOTS)]
        tab_step = sem("tab_step")
        tab_ok = sem("tab_ok")
        fill_in = sem("fill_in")
        b_load = [sem(f"b_load{s}") for s in range(SLOTS)]
        yhat_ok = sem("yhat_ok")
        yt_ps = sem("yt_ps")
        yhi_sb = sem("yhi_sb")
        ylo_sb = sem("ylo_sb")
        bh_ps = sem("bh_ps")
        bh_sb = sem("bh_sb")
        y_ps = sem("y_ps")
        res_ok = sem("res_ok")
        stored = [sem(f"stored{s}") for s in range(2)]

        block = ctx.enter_context(nc.Block())

        def after(eng, s, n):
            if not (isinstance(n, int) and n <= 0):
                eng.wait_ge(s, n)

        out_rows = out.rearrange("b n c -> (b n) c")
        x_view = x.rearrange("(g t) p f -> g p t f", t=T)
        adj_view = adj.rearrange("(g t) p m -> g p t m", t=T)

        A_FIRST, A_LOOP, A_END = -1, 3, GROUPS - 1

        def phase_a(eng, body):
            for c in range(A_FIRST, A_LOOP):
                body(0, c)
            with eng.Fori(0, (A_END - A_LOOP) // 4) as k:
                for j in range(4):
                    body(k, A_LOOP + j)
            for c in range(A_END, A_END + 4):
                body(0, c)

        def group(k, c):
            if isinstance(k, int) and not 0 <= c < GROUPS:
                return None
            return Step(k, c)

        B_LOOP, B_END = 1, QUADS - 5
        assert (A_END - A_LOOP) % 4 == 0 and (B_END - B_LOOP) % 4 == 0

        def phase_b(eng, body):
            for c in range(-1, B_LOOP):
                body(0, c)
            with eng.Fori(0, (B_END - B_LOOP) // 4) as k:
                for j in range(4):
                    body(k, B_LOOP + j)
            for c in range(B_END, QUADS + 1):
                body(0, c)

        def quad(k, c):
            if isinstance(k, int) and not 0 <= c < QUADS:
                return None
            return Step(k, c)

        W_LOADS = 7 + HC
        N_FILL = E + 1

        @block.sync
        def _(sp):
            def load_group(g):
                after(sp, x1_ok, g.n - 1)
                sp.dma_start(x_in[:, g.slot2], x_view[bass.ds(g.n, 1)].rearrange("a p t f -> (a p) t f")
                             ).then_inc(x_load[g.slot2], 16)
                after(sp, at_ps, g.n - 1)
                after(sp, stat1, g.n - 1)
                sp.dma_start(adj_in[:, g.slot2], adj_view[bass.ds(g.n, 1)].rearrange("a p t f -> (a p) t f")
                             ).then_inc(a_load[g.slot2], 16)

            load_group(Step(0, 0))
            sp.dma_start(gnn_w_sb[:], gnn_w).then_inc(w_in, 16)
            sp.dma_start(gnn_b_all[:], gnn_b.rearrange("(a b f) -> a b f", a=1, b=1).to_broadcast([P, T, D])
                         ).then_inc(w_in, 16)
            load_group(Step(0, 1))
            sp.dma_start(w1_sb[:], w1).then_inc(w_in, 16)
            sp.dma_start(b1_col[:], b1.rearrange("(c p) -> p c", p=P), allow_slow_non_contiguous=True
                         ).then_inc(w_in, 16)
            sp.dma_start(wg_in[:], wg.rearrange("(c p) e -> p c e", p=P)).then_inc(w_in, 16)
            after(sp, const_pool, 1)
            sp.dma_start(bg_col[0:E], bg.rearrange("(e a) -> e a", a=1)).then_inc(w_in, 16)
            sp.dma_start(bd_row[:], bd.rearrange("(a e) c -> a (e c)", a=1)).then_inc(w_in, 16)
            for c in range(HC):
                sp.dma_start(wd_sb[:, c].rearrange("p (e o) -> p e o", e=E),
                             wd[:, c * P:(c + 1) * P].rearrange("e p o -> p e o")).then_inc(w_in, 16)

            after(sp, v1_setup, 5)
            for part in range(3):
                sp.dma_start(bd3[part:part + 1], bd_part[:, part]).then_inc(bd_in, 16)

            def body(k, c):
                g = group(k, c + 1)
                if g and not (g.fixed and g.n < 2):
                    load_group(g)

            phase_a(sp, body)

            sp.wait_ge(tab_ok, 1)
            for e in range(E):
                r = sp.value_load(fill_row[0:1, e:e + 1], min_val=0, max_val=E * REGION - P)
                sp.dma_start(table[bass.ds(r, P)], filler[:]).then_inc(fill_in, 16)
            sp.dma_start(table[E * REGION:E * REGION + P], filler[:]).then_inc(fill_in, 16)
            sp.wait_ge(fill_in, 16 * N_FILL)
            for s in range(SLOTS):
                sp.wait_ge(scattered[s], 16 * T * (GROUPS // SLOTS))

            def load_quad(q):
                if not (q.fixed and q.n < 4):
                    after(sp, stored[q.slot2], 16 * T * (q.nth2 - 1))
                for t in range(T):
                    r = sp.value_load(tile_row[0:1, bass.ds(T * q.n + t, 1)], min_val=0, max_val=E * REGION)
                    sp.dma_start(rows_b[:, q.slot4, t], table[bass.ds(r, P)]).then_inc(b_load[q.slot4], 16)

            load_quad(Step(0, 0))
            load_quad(Step(0, 1))

            def body(k, c):
                q = quad(k, c + 1)
                if q and not (q.fixed and q.n < 2):
                    load_quad(q)

            phase_b(sp, body)

        @block.gpsimd
        def _(pool):
            pool.memset(bg_col[:], 0.0).then_inc(const_pool, 1)
            pool.memset(minus_half[:], -0.5)
            pool.memset(pace[:], 0.0)
            pool.memset(ident[:], 0.0)
            pool.memset(gate_sum[:], 0.0)
            pool.memset(earlier[:], 1.0)
            pool.memset(ones[:], 1.0)
            pool.memset(wg_sb[:], 0.0)
            pool.memset(upto[:], 1.0)
            pool.memset(filler[:], 0.0)
            pool.iota(region_i[:], [[REGION // P, E]], base=0, channel_multiplier=0)
            pool.iota(tile_no_i[:], [[1, TILES]], base=0, channel_multiplier=0)
            pool.iota(seed_tok[:], [[P, T]], base=0, channel_multiplier=1)
            pool.iota(first_wins[:], [[0, T], [-1, E]], base=E, channel_multiplier=0,
                      allow_small_or_imprecise_dtypes=True).then_inc(const_pool, 1)
            pool.wait_ge(const_pool, 2)
            pool.affine_select(out=ident[:], in_=ident[:], compare_op=ALU.not_equal, fill=1.0, base=0,
                               pattern=[[-1, P]], channel_multiplier=1)
            pool.affine_select(out=earlier[:], in_=earlier[:], compare_op=ALU.is_gt, fill=0.0, base=0,
                               pattern=[[1, P]], channel_multiplier=-1)
            pool.affine_select(out=upto[:], in_=upto[:], compare_op=ALU.is_ge, fill=0.0, base=0,
                               pattern=[[1, E], [-1, E]], channel_multiplier=0)
            for c in range(HC):
                if c:
                    pool.wait_ge(const_pool, 2 + c)
                pool.affine_select(out=gate_sum[:], in_=gate_sum[:], compare_op=ALU.not_equal, fill=1.0,
                                   base=-32 * c, pattern=[[-1, E]], channel_multiplier=1
                                   ).then_inc(const_pool, 1)
            pool.wait_ge(w_in, 16 * W_LOADS)
            pool.tensor_copy(wg_sb[:, :, 0:E], wg_in[:]).then_inc(const_pool, 1)

            def powers1(g):
                pool.wait_ge(stat1, g.n + 1)
                after(pool, xhat_ok, g.n)
                pool.tensor_tensor(pow_out[:], pow_in[:], minus_half[:], ALU.pow).then_inc(pow1, 1)

            def powers2(g):
                pool.wait_ge(stat2, g.n + 1)
                pool.tensor_tensor(rows[:, g.slot4, :, C_RSTD], var2[:], minus_half[:, 0:T], ALU.pow
                                   ).then_inc(pow2, 1)

            def scatter(g):
                pool.wait_ge(row_ok, g.n + 1)
                pool.tensor_tensor(pace_out[:, g.slot4:g.slot4 + 1], pace[:], pace[:], ALU.add).then_inc(paced, 1)
                for t in range(T):
                    pool.indirect_dma_start(table, bass.IndirectOffsetOnAxis(ap=index[:, g.slot2, t:t + 1], axis=0),
                                            rows[:, g.slot4, t], None).then_inc(scattered[g.slot4], 16)

            def body(k, c):
                if g := group(k, c - 1):
                    powers2(g)
                if g := group(k, c + 1):
                    powers1(g)
                if g := group(k, c - 3):
                    scatter(g)

            phase_a(pool, body)

            last_token = pool.to_reg(TOKENS - 1)

            def store(q):
                pool.wait_ge(res_ok, q.n + 1)
                after(pool, paced, GROUPS + q.n)
                pool.tensor_tensor(pace_out[:, q.slot4:q.slot4 + 1], pace[:], pace[:], ALU.add).then_inc(paced, 1)
                for t in range(T):
                    pool.indirect_dma_start(
                        out_rows, bass.IndirectOffsetOnAxis(
                            ap=rows_b[:, q.slot4, t, C_TOK:C_TOK + 1].bitcast(I32), axis=0),
                        result[:, q.slot2, t], None, bounds_check=last_token, oob_is_err=False,
                    ).then_inc(stored[q.slot2], 16)

            def body(k, c):
                if q := quad(k, c - 1):
                    store(q)

            phase_b(pool, body)
            for s in range(2):
                pool.wait_ge(stored[s], 16 * T * (QUADS // 2))

        @block.tensor
        def _(pe):
            pe.wait_ge(const_pool, 3 + HC)
            pe.wait_ge(w_in, 16 * W_LOADS)
            pe.transpose(ps_f[:, 0:P], gnn_w_sb[:], ident[:]).then_inc(wt_ps, 1)
            pe.wait_ge(wt_sb, 1)
            pe.wait_ge(const_dve, 1)

            def adj_transposes(g):
                pe.wait_ge(a_load[g.slot2], 16 * (g.nth2 + 1))
                after(pe, at_sb, g.n)
                for t in range(T):
                    last = pe.transpose(ps_a[:, t * P:(t + 1) * P], adj_in[:, g.slot2, t], ident[:])
                last.then_inc(at_ps, 1)

            def xhat_transposes(g):
                pe.wait_ge(xhat_ok, g.n + 1)
                after(pe, xt_sb, g.n)
                after(pe, x2t_sb, g.n - 1)
                for t in range(T):
                    last = pe.transpose(ps_x[:, t * P:(t + 1) * P], xhat[:, g.slot2, t], ident[:])
                last.then_inc(xt_ps, 1)

            def features(g):
                pe.wait_ge(xt_sb, g.n + 1)
                after(pe, f_sb, g.n)
                for t in range(T):
                    last = pe.matmul(ps_f[:, t * D:(t + 1) * D], xhat_t[:, t * P:(t + 1) * P], gnn_wt[:],
                                     start=True, stop=True)
                last.then_inc(f_ps, 1)

            def aggregate(g):
                pe.wait_ge(f_sb, g.n + 1)
                pe.wait_ge(at_sb, g.n + 1)
                after(pe, agg_ok, g.n)
                for t in range(T):
                    last = pe.matmul(ps_u[:, t * D:(t + 1) * D], adj_t[:, t], feats[:, t], start=True, stop=True)
                last.then_inc(u_ps, 1)

            def x2_transposes(g):
                pe.wait_ge(x2hat_ok, g.n + 1)
                pe.wait_ge(xt_sb, g.n + 1)
                if not (g.fixed and g.n == GROUPS - 1):
                    pe.wait_ge(xt_sb, g.n + 2)
                after(pe, x2t_sb, g.n)
                for t in range(T):
                    last = pe.transpose(ps_x[:, t * P:(t + 1) * P], x2hat[:, t], ident[:])
                last.then_inc(x2t_ps, 1)

            def hidden_chunk(g, c):
                if c == 0:
                    pe.wait_ge(x2t_sb, g.n + 1)
                after(pe, h_sb, HC * g.n + c - 1)
                pe.matmul(ps_h[c % 2][:], w1_sb[:, c * P:(c + 1) * P], x2hat_t[:, g.slot2], start=True, stop=True
                          ).then_inc(h_ps, 1)

            def gate(g):
                pe.wait_ge(h_sb, HC * (g.n + 1))
                after(pe, lt_sb, g.n)
                for c in range(HC):
                    last = pe.matmul(ps_g[32 * c:32 * c + 32], wg_sb[:, c], hidden[:, 0, c], start=True, stop=True)
                last.then_inc(g_ps, 1)

            def logits(g):
                pe.wait_ge(lt_sb, g.n + 1)
                after(pe, row_ok, g.n)
                for t in range(T):
                    last = pe.matmul(logit_ps[:, t], logits_t[:, t * P:(t + 1) * P], gate_sum[:], start=True, stop=True)
                last.then_inc(l_ps, 1)

            def ranks(g):
                pe.wait_ge(chosen_ok, g.n + 1)
                pe.matmul(rank_ps[:, 0:T], earlier[:], chosen[:], start=True, stop=False, skip_group_check=True)
                for t in range(T):
                    n = T - t
                    last = pe.matmul(rank_ps[:, t + 1:T + 1], ones[:],
                                     chosen[:, t:t + 1].to_broadcast([P, n, E]), start=False, stop=(t == T - 1),
                                     skip_group_check=True)
                last.then_inc(rank_ok, 1)

            def body(k, c):
                cur, two, three, one = group(k, c), group(k, c - 2), group(k, c - 3), group(k, c - 1)
                if cur:
                    xhat_transposes(cur)
                    adj_transposes(cur)
                if three:
                    gate(three)
                if cur:
                    features(cur)
                if three:
                    logits(three)
                if two:
                    hidden_chunk(two, 0)
                if cur:
                    aggregate(cur)
                if three:
                    ranks(three)
                if two:
                    hidden_chunk(two, 1)
                if one:
                    x2_transposes(one)
                if two:
                    hidden_chunk(two, 2)
                    hidden_chunk(two, 3)

            phase_a(pe, body)

            pe.wait_ge(bd_in, 48)
            pe.wait_ge(tab_ok, 1)

            def yhat_transposes(q):
                pe.wait_ge(yhat_ok, q.n + 1)
                after(pe, ylo_sb, q.n)
                for t in range(T):
                    last = pe.transpose(ps_x[:, t * P:(t + 1) * P], yhat[:, t], ident[:])
                last.then_inc(yt_ps, 1)

            def hidden_b(q, c):
                if c == 0:
                    pe.wait_ge(yhi_sb, q.n + 1)
                    pe.wait_ge(ylo_sb, q.n + 1)
                after(pe, bh_sb, HC * q.n + c - 1)
                w = slice(c * P, (c + 1) * P)
                pe.matmul(ps_h[c % 2][:], w1_hi[:, w], yhat_hi[:, q.slot2], start=True, stop=False)
                pe.matmul(ps_h[c % 2][:], w1_hi[:, w], yhat_lo[:, q.slot2], start=False, stop=False)
                pe.matmul(ps_h[c % 2][:], w1_lo[:, w], yhat_hi[:, q.slot2], start=False, stop=True
                          ).then_inc(bh_ps, 1)

            def expert(q, t):
                col = pe.value_load(tile_col[0:1, bass.ds(T * q.n + t, 1)], min_val=0, max_val=(E - 1) * D)
                if t == 0:
                    pe.wait_ge(bh_sb, HC * (q.n + 1))
                after(pe, res_ok, q.n)
                pe.matmul(ps_y[t][:, 0:D], ones[0:3, :], bd3[:, bass.ds(col, D)], start=True, stop=False)
                for c in range(HC):
                    last = pe.matmul(ps_y[t][:, 0:D], hidden[:, q.slot2, c, t * P:(t + 1) * P],
                                     wd_sb[:, c, bass.ds(col, D)], start=False, stop=(c == HC - 1))
                last.then_inc(y_ps, 1)

            def body(k, c):
                prev, cur, nxt = quad(k, c - 1), quad(k, c), quad(k, c + 1)
                if cur:
                    hidden_b(cur, 0)
                if nxt:
                    yhat_transposes(nxt)
                if cur:
                    hidden_b(cur, 1)
                if prev:
                    expert(prev, 0)
                    expert(prev, 1)
                if cur:
                    hidden_b(cur, 2)
                if prev:
                    expert(prev, 2)
                    expert(prev, 3)
                if cur:
                    hidden_b(cur, 3)

            phase_b(pe, body)

        @block.scalar
        def _(act):
            def adj_copy(g):
                act.wait_ge(at_ps, g.n + 1)
                act.wait_ge(dinv_ok, g.n + 1)
                after(act, u_ps, g.n)
                for t in range(T):
                    last = act.activation(adj_t[:, t], ps_a[:, t * P:(t + 1) * P], ACT.Copy,
                                          scale=dinv[:, g.slot2, t:t + 1])
                last.then_inc(at_sb, 1)

            def xhat_copy(g):
                act.wait_ge(xt_ps, g.n + 1)
                after(act, f_ps, g.n)
                act.copy(xhat_t[:], ps_x[:]).then_inc(xt_sb, 1)

            def relu(g):
                act.wait_ge(u_ps, g.n + 1)
                after(act, x1_ok, g.n)
                for t in range(T):
                    last = act.activation(agg[:, t], ps_u[:, t * D:(t + 1) * D], ACT.Relu,
                                          scale=dinv[:, g.slot2, t:t + 1])
                last.then_inc(agg_ok, 1)

            def x2_copy(g):
                act.wait_ge(x2t_ps, g.n + 1)
                after(act, h_ps, HC * (g.n - 1))
                act.copy(x2hat_t[:, g.slot2], ps_x[:]).then_inc(x2t_sb, 1)

            def gelu(g, c):
                act.wait_ge(h_ps, HC * g.n + c + 1)
                after(act, g_ps, g.n)
                act.activation(hidden[:, 0, c], ps_h[c % 2][:], ACT.Gelu, bias=b1_col[:, c:c + 1]).then_inc(h_sb, 1)

            def logits_copy(g):
                act.wait_ge(g_ps, g.n + 1)
                after(act, l_ps, g.n)
                act.activation(logits_t[:], ps_g[:], ACT.Identity, bias=bg_col[:, 0:1]).then_inc(lt_sb, 1)

            def tanh(g):
                act.wait_ge(v6_step, 4 * g.n + 2)
                after(act, row_ok, g.n)
                act.activation(tanh_half[:], below[:], ACT.Tanh, scale=0.5).then_inc(tanh_ok, 1)

            act.wait_ge(w_in, 16 * W_LOADS)

            def body(k, c):
                cur, two, three, one = group(k, c), group(k, c - 2), group(k, c - 3), group(k, c - 1)
                if cur:
                    xhat_copy(cur)
                    adj_copy(cur)
                if three:
                    logits_copy(three)
                if two:
                    gelu(two, 0)
                if cur:
                    relu(cur)
                if three:
                    tanh(three)
                if two:
                    gelu(two, 1)
                if one:
                    x2_copy(one)
                if two:
                    gelu(two, 2)
                    gelu(two, 3)

            phase_a(act, body)

            def yhat_copy(q):
                act.wait_ge(yt_ps, q.n + 1)
                after(act, bh_ps, HC * (q.n - 1))
                act.copy(yhat_hi[:, q.slot2], ps_x[:]).then_inc(yhi_sb, 1)

            def gelu_b(q, c):
                act.wait_ge(bh_ps, HC * q.n + c + 1)
                after(act, y_ps, T * (q.n - 1))
                act.activation(hidden[:, q.slot2, c], ps_h[c % 2][:], ACT.Gelu, bias=b1_col[:, c:c + 1]
                               ).then_inc(bh_sb, 1)

            def body(k, c):
                cur, nxt = quad(k, c), quad(k, c + 1)
                if cur:
                    gelu_b(cur, 0)
                if nxt:
                    yhat_copy(nxt)
                if cur:
                    gelu_b(cur, 1)
                    gelu_b(cur, 2)
                    gelu_b(cur, 3)

            phase_b(act, body)

        @block.vector
        def _(dve):
            dve.wait_ge(w_in, 16 * W_LOADS)
            dve.wait_ge(const_pool, 2)
            dve.tensor_copy(w1_hi[:], w1_sb[:])
            dve.tensor_copy(tok_f[:], seed_tok[:])
            dve.tensor_copy(tile_no[:], tile_no_i[:])
            dve.tensor_scalar(base[:], region_i[:], float(P), None, ALU.mult)
            dve.tensor_scalar(region0[:], region_i[:], float(P), None, ALU.mult)
            dve.tensor_copy(bd_part[:, 0], bd_row[:]).then_inc(v1_setup, 1)
            dve.wait_ge(v1_setup, 1)
            dve.tensor_tensor(w1_lo[:], w1_sb[:], w1_hi[:].bitcast(F32), ALU.subtract).then_inc(const_dve, 1)
            dve.tensor_tensor(bd_rest[:], bd_row[:], bd_part[:, 0], ALU.subtract).then_inc(v1_setup, 1)
            dve.wait_ge(v1_setup, 2)
            dve.tensor_copy(bd_part[:, 1], bd_rest[:]).then_inc(v1_setup, 1)
            dve.wait_ge(v1_setup, 3)
            dve.tensor_tensor(bd_row[:], bd_rest[:], bd_part[:, 1], ALU.subtract).then_inc(v1_setup, 1)
            dve.wait_ge(v1_setup, 4)
            dve.tensor_copy(bd_part[:, 2], bd_row[:]).then_inc(v1_setup, 1)
            dve.tensor_scalar(filler[:, C_TOK:C_TOK + 1].bitcast(I32), base[:, 0:1], 0.0, float(TOKENS),
                              ALU.mult, ALU.add).then_inc(v1_setup, 1)
            dve.wait_ge(wt_ps, 1)
            dve.tensor_copy(gnn_wt[:], ps_f[:, 0:P]).then_inc(wt_sb, 1)

            def moments(bn, mean, step, done):
                even, odd = bn[:, :, 0:3], bn[:, :, 3:6]
                dve.tensor_tensor(m_sum[:], even[:, :, 1], odd[:, :, 1], ALU.add)
                dve.tensor_tensor(m_diff[:], even[:, :, 1], odd[:, :, 1], ALU.subtract)
                dve.tensor_tensor(m_sq[:], even[:, :, 2], odd[:, :, 2], ALU.add).then_inc(step, 1)
                dve.wait_ge(step, done + 1)
                dve.tensor_scalar(mean[:], m_sum[:], 0.5, None, ALU.mult)
                dve.scalar_tensor_tensor(m_between[:], m_diff[:], 0.25, m_diff[:], ALU.mult, ALU.mult)
                dve.tensor_scalar(m_within[:], m_sq[:], 1.0 / D, EPS, ALU.mult, ALU.add).then_inc(step, 1)

            def statistics1(g):
                dve.wait_ge(x_load[g.slot2], 16 * (g.nth2 + 1))
                for t in range(T):
                    last = dve.bn_stats(bn1[:, t], x_in[:, g.slot2, t])
                last.then_inc(v1_step, 1)
                dve.wait_ge(a_load[g.slot2], 16 * (g.nth2 + 1))
                after(dve, dinv_ok, g.n)
                dve.tensor_reduce(deg[:], adj_in[:, g.slot2], AX_X, ALU.add).then_inc(v1_step, 1)
                dve.wait_ge(v1_step, 4 * g.n + 1)
                after(dve, xhat_ok, g.n)
                moments(bn1, mean1, v1_step, 4 * g.n + 2)
                after(dve, pow1, g.n)
                dve.scalar_tensor_tensor(pow_in[:, 0:T], deg[:], 0.0, deg[:], ALU.is_equal, ALU.add)
                dve.wait_ge(v1_step, 4 * g.n + 4)
                dve.tensor_tensor(pow_in[:, T:2 * T], m_within[:], m_between[:], ALU.add).then_inc(stat1, 1)

            def normalize1(g):
                dve.wait_ge(pow1, g.n + 1)
                after(dve, agg_ok, g.n - 1)
                after(dve, at_sb, g.n - 1)
                dve.scalar_tensor_tensor(dinv[:, g.slot2], deg[:], 0.0, pow_out[:, 0:T], ALU.not_equal, ALU.mult
                                         ).then_inc(dinv_ok, 1)
                after(dve, xt_ps, g.n - 1)
                for t in range(T):
                    last = dve.tensor_scalar(xhat[:, g.slot2, t], x_in[:, g.slot2, t], mean1[:, t:t + 1],
                                             pow_out[:, T + t:T + t + 1], ALU.subtract, ALU.mult)
                last.then_inc(xhat_ok, 1)

            def add_bias(g):
                dve.wait_ge(f_ps, g.n + 1)
                after(dve, u_ps, g.n)
                dve.tensor_tensor(feats[:], ps_f[:].rearrange("p (t d) -> p t d", t=T), gnn_b_all[:], ALU.add
                                  ).then_inc(f_sb, 1)

            def residual(g):
                dve.wait_ge(agg_ok, g.n + 1)
                after(dve, scattered[g.slot4], 16 * T * g.nth4)
                dve.tensor_tensor(rows[:, g.slot4, :, 0:D], agg[:], x_in[:, g.slot2], ALU.add).then_inc(x1_ok, 1)
                dve.wait_ge(x1_ok, g.n + 1)
                for t in range(T):
                    last = dve.bn_stats(bn2[:, t], rows[:, g.slot4, t, 0:D])
                last.then_inc(v4_step, 1)
                dve.wait_ge(v4_step, 3 * g.n + 1)
                after(dve, x2hat_ok, g.n)
                moments(bn2, mean2, v4_step, 3 * g.n + 1)
                dve.wait_ge(v4_step, 3 * g.n + 3)
                after(dve, pow2, g.n)
                dve.tensor_tensor(var2[:], m_within[:], m_between[:], ALU.add).then_inc(stat2, 1)

            def normalize2(g):
                dve.wait_ge(pow2, g.n + 1)
                after(dve, x2t_ps, g.n)
                rstd = rows[:, g.slot4, :, C_RSTD]
                dve.scalar_tensor_tensor(rows[:, g.slot4, :, C_NMR], mean2[:], -1.0, rstd, ALU.mult, ALU.mult
                                         ).then_inc(v5_step, 1)
                for t in range(T):
                    last = dve.tensor_scalar(x2hat[:, t], rows[:, g.slot4, t, 0:D], mean2[:, t:t + 1],
                                             rows[:, g.slot4, t, C_RSTD:C_RSTD + 1], ALU.subtract, ALU.mult)
                last.then_inc(x2hat_ok, 1)

            def choose(g):
                dve.wait_ge(l_ps, g.n + 1)
                dve.tensor_reduce(top[:], logit_ps, AX_X, ALU.max).then_inc(v6_step, 1)
                dve.wait_ge(v6_step, 4 * g.n + 1)
                after(dve, tanh_ok, g.n)
                dve.tensor_tensor(below[:], logit_ps, top[:].rearrange("p (t a) -> p t a", a=1).to_broadcast([P, T, E]),
                                  ALU.subtract).then_inc(v6_step, 1)
                dve.wait_ge(v6_step, 4 * g.n + 2)
                dve.scalar_tensor_tensor(cand[:].rearrange("p t e -> p (t e)"), below[:].rearrange("p t e -> p (t e)"),
                                         0.0, first_wins[:].rearrange("p t e -> p (t e)"), ALU.is_equal, ALU.mult
                                         ).then_inc(v6_step, 1)
                dve.wait_ge(v6_step, 4 * g.n + 3)
                dve.tensor_reduce(best[:], cand[:], AX_X, ALU.max).then_inc(v6_step, 1)
                dve.wait_ge(v6_step, 4 * g.n + 4)
                dve.tensor_tensor(chosen[:], cand[:], best[:].rearrange("p (t a) -> p t a", a=1).to_broadcast([P, T, E]),
                                  ALU.is_equal).then_inc(chosen_ok, 1)

            def finish_rows(g):
                dve.wait_ge(tanh_ok, g.n + 1)
                dve.tensor_scalar(soft[:], tanh_half[:], -1.0, 1.0, ALU.mult, ALU.add).then_inc(v7_step, 1)
                dve.wait_ge(rank_ok, g.n + 1)
                dve.tensor_tensor(place[:], rank_ps[:, 0:T], base[:].rearrange("p (a e) -> p a e", a=1).to_broadcast(
                    [P, T, E]), ALU.add).then_inc(v7_step, 1)
                dve.wait_ge(v7_step, 8 * g.n + 1)
                dve.reciprocal(soft_r[:], soft[:]).then_inc(v7_step, 1)
                dve.wait_ge(v7_step, 8 * g.n + 2)
                dve.tensor_tensor(base[:], base[:], rank_ps[:, T], ALU.add).then_inc(v7_step, 1)
                dve.tensor_tensor(place_own[:], place[:], chosen[:], ALU.mult).then_inc(v7_step, 1)
                dve.wait_ge(v7_step, 8 * g.n + 3)
                dve.tensor_reduce(soft_sum[:], soft_r[:], AX_X, ALU.add).then_inc(v7_step, 1)
                dve.tensor_copy(rows[:, g.slot4, :, C_TOK].bitcast(I32), tok_f[:])
                dve.wait_ge(v7_step, 8 * g.n + 5)
                dve.tensor_reduce(place_sum[:], place_own[:], AX_X, ALU.add).then_inc(v7_step, 1)
                dve.wait_ge(v7_step, 8 * g.n + 6)
                dve.tensor_scalar(denom[:], soft_sum[:], 2.0, -float(E), ALU.mult, ALU.add).then_inc(v7_step, 1)
                dve.wait_ge(v7_step, 8 * g.n + 7)
                after(dve, scattered[(g.slot4 + 2) % 4], 16 * T * g.uses_back2)
                dve.tensor_copy(index[:, g.slot2], place_sum[:])
                dve.wait_ge(v7_step, 8 * g.n + 8)
                dve.tensor_scalar(tok_f[:], tok_f[:], float(GT), None, ALU.add)
                dve.reciprocal(rows[:, g.slot4, :, C_PROB], denom[:]).then_inc(row_ok, 1)

            def body(k, c):
                cur, nxt, three, one = group(k, c), group(k, c + 1), group(k, c - 3), group(k, c - 1)
                if cur:
                    add_bias(cur)
                if three:
                    choose(three)
                if one:
                    normalize2(one)
                if nxt:
                    statistics1(nxt)
                if three:
                    finish_rows(three)
                if nxt:
                    normalize1(nxt)
                if cur:
                    residual(cur)

            phase_a(dve, body)

            steps = [0]

            def link(ins):
                steps[0] += 1
                ins.then_inc(tab_step, 1)
                dve.wait_ge(tab_step, steps[0])

            dve.wait_ge(row_ok, GROUPS)
            dve.tensor_copy(fill_row[:], base[0:1, :])
            link(dve.tensor_tensor(count_f[:], base[0:1, :], region0[0:1, :], ALU.subtract))
            link(dve.tensor_scalar(count_i[:], count_f[:], float(P - 1), None, ALU.add))
            link(dve.tensor_scalar(ntile_i[:], count_i[:], P.bit_length() - 1, None, ALU.logical_shift_right))
            link(dve.tensor_copy(ntile_f[:], ntile_i[:]))
            link(dve.tensor_tensor(ntile_upto[:], upto[:], ntile_f[:].rearrange("p (a e) -> p a e", a=1).to_broadcast(
                [1, E, E]), ALU.mult))
            link(dve.tensor_scalar(jump[:], ntile_f[:], -float(P), float(REGION), ALU.mult, ALU.add))
            link(dve.tensor_reduce(last_tile[:], ntile_upto[:], AX_X, ALU.add))
            link(dve.tensor_tensor(passed[:], tile_no[:].rearrange("p (j a) -> p j a", a=1).to_broadcast([1, TILES, E]),
                                   last_tile[:].rearrange("p (a e) -> p a e", a=1).to_broadcast([1, TILES, E]),
                                   ALU.is_ge))
            link(dve.tensor_tensor(jumped[:], passed[:], jump[:].rearrange("p (a e) -> p a e", a=1).to_broadcast(
                [1, TILES, E]), ALU.mult))
            link(dve.tensor_reduce(tile_e[:], passed[:], AX_X, ALU.add))
            link(dve.tensor_reduce(tile_r[:], jumped[:], AX_X, ALU.add))
            link(dve.scalar_tensor_tensor(tile_r2[:], tile_no[:], float(P), tile_r[:], ALU.mult, ALU.add))
            link(dve.tensor_scalar(tile_row[:], tile_r2[:], float(E * REGION), None, ALU.min))
            link(dve.tensor_scalar(tile_col[:], tile_e[:], float(E - 1), float(D), ALU.min, ALU.mult))
            dve.wait_ge(v1_setup, 6)
            dve.tensor_copy(tile_e[:], tile_e[:]).then_inc(tab_ok, 1)

            def normalize_b(q):
                dve.wait_ge(b_load[q.slot4], 16 * T * (q.nth4 + 1))
                after(dve, yt_ps, q.n)
                for t in range(T):
                    r = rows_b[:, q.slot4, t]
                    last = dve.tensor_scalar(yhat[:, t], r[:, 0:D], r[:, C_RSTD:C_RSTD + 1], r[:, C_NMR:C_NMR + 1],
                                             ALU.mult, ALU.add)
                last.then_inc(yhat_ok, 1)

            def low_part(q):
                dve.wait_ge(yhi_sb, q.n + 1)
                dve.tensor_tensor(yhat_lo[:, q.slot2], ps_x[:], yhat_hi[:, q.slot2].bitcast(F32), ALU.subtract
                                  ).then_inc(ylo_sb, 1)

            def results(q, t):
                dve.wait_ge(y_ps, T * q.n + t + 1)
                if t == 0 and not (q.fixed and q.n < 2):
                    after(dve, stored[q.slot2], 16 * T * q.nth2)
                r = rows_b[:, q.slot4, t]
                last = dve.scalar_tensor_tensor(result[:, q.slot2, t], ps_y[t][:, 0:D], r[:, C_PROB:C_PROB + 1],
                                                r[:, 0:D], ALU.mult, ALU.add)
                if t == T - 1:
                    last.then_inc(res_ok, 1)

            def body(k, c):
                prev, nxt, far = quad(k, c - 1), quad(k, c + 1), quad(k, c + 2)
                if nxt and nxt.fixed and nxt.n == 0:
                    normalize_b(nxt)
                if nxt:
                    low_part(nxt)
                if far:
                    normalize_b(far)
                if prev:
                    for t in range(T):
                        results(prev, t)

            phase_b(dve, body)


_INS = ["x", "adj", "L0_gnn_W", "L0_gnn_b", "L0_ffn_W1", "L0_ffn_b1", "L0_ffn_Wg", "L0_ffn_bg", "L0_ffn_Wd",
        "L0_ffn_bd"]


def kernel(**inputs):
    import numpy as _np
    import concourse.bacc as _bacc
    from concourse import mybir as _mybir
    from concourse.bass_utils import run_bass_kernel_spmd as _run

    nc = _bacc.Bacc("TRN2", target_bir_lowering=False, num_devices=1)
    arrays, args = {}, []
    for name in _INS:
        a = _np.ascontiguousarray(inputs[name])
        arrays[f"in_{name}_dram"] = a
        args.append(nc.dram_tensor(f"in_{name}_dram", a.shape, _mybir.dt.from_np(a.dtype), kind="ExternalInput").ap())
    result = nc.dram_tensor("out_0_dram", (GRAPHS, P, D), F32, kind="ExternalOutput").ap()
    moe_gnn_kernel(nc, *args, result)
    r = _run(nc, [arrays], core_ids=[0])
    return r.results[0]["out_0_dram"]
```

```python
from contextlib import ExitStack

import concourse.bass as bass
from concourse import mybir

ALU = mybir.AluOpType
ACT = mybir.ActivationFunctionType
AX_X = mybir.AxisListType.X
F32 = mybir.dt.float32
F32R = mybir.dt.float32r
BF16 = mybir.dt.bfloat16
I32 = mybir.dt.int32

P = 128
GRAPHS = 128
TOKENS = GRAPHS * P
D = 128
HID = 512
HC = HID // P
E = 8
T = 4
GROUPS = GRAPHS // T
GT = T * P
EPS = 1e-5
ROW = D + 4
C_NMR, C_RSTD, C_PROB, C_TOK = D, D + 1, D + 2, D + 3
REGION = TOKENS + P
TILES = TOKENS // P + E
QUADS = TILES // T
SLOTS = 4


class Step:

    def __init__(self, k, c):
        self.n = 4 * k + c
        self.slot4, self.slot2 = c % 4, c % 2
        self.nth4, self.nth2 = k + c // 4, 2 * k + c // 2
        self.uses_back2 = k + (c + 2) // 4
        self.fixed = isinstance(k, int)


def moe_gnn_kernel(nc, x, adj, gnn_w, gnn_b, w1, b1, wg, bg, wd, bd, out):
    with ExitStack() as ctx:
        def sb(name, shape, dt=F32):
            return ctx.enter_context(nc.sbuf_tensor(name, shape, dt))

        def bank(name, shape=(P, 512), dt=F32):
            return ctx.enter_context(nc.psum_tensor(name, list(shape), dt))

        def sem(name):
            return ctx.enter_context(nc.semaphore(name))

        table = nc.dram_tensor("table", [E * REGION + P, ROW], F32).ap()

        ident = sb("ident", [P, P])
        earlier = sb("earlier", [P, P], BF16)
        ones = sb("ones", [P, P], BF16)
        gate_sum = sb("gate_sum", [P, E])
        first_wins = sb("first_wins", [P, T, E])
        seed_tok = sb("seed_tok", [P, T], I32)
        tok_f = sb("tok_f", [P, T])
        minus_half = sb("minus_half", [P, 2 * T])
        gnn_w_sb = sb("gnn_w_sb", [P, D])
        gnn_wt = sb("gnn_wt", [P, D])
        gnn_b_all = sb("gnn_b_all", [P, T, D])
        w1_sb = sb("w1_sb", [P, HID])
        w1_hi = sb("w1_hi", [P, HID], F32R)
        w1_lo = sb("w1_lo", [P, HID], F32R)
        b1_col = sb("b1_col", [P, HC])
        wg_sb = sb("wg_sb", [P, HC, 32])
        wg_in = sb("wg_in", [P, HC, E])
        bg_col = sb("bg_col", [P, 1])
        wd_sb = sb("wd_sb", [P, HC, E * D])
        bd_row = sb("bd_row", [1, E * D])
        bd_rest = sb("bd_rest", [1, E * D])
        bd_part = sb("bd_part", [1, 3, E * D], BF16)
        bd3 = sb("bd3", [3, E * D], BF16)

        x_in = sb("x_in", [P, SLOTS, T, D])
        adj_in = sb("adj_in", [P, SLOTS, T, P])
        bn1 = sb("bn1", [P, T, 6])
        mean1 = sb("mean1", [P, T])
        m_sum = sb("m_sum", [P, T])
        m_diff = sb("m_diff", [P, T])
        m_sq = sb("m_sq", [P, T])
        m_between = sb("m_between", [P, T])
        m_within = sb("m_within", [P, T])
        pace = sb("pace", [1, 1])
        pace_out = sb("pace_out", [1, SLOTS])
        deg = sb("deg", [P, T])
        pow_in = sb("pow_in", [P, 2 * T])
        pow_out = sb("pow_out", [P, 2 * T])
        dinv = sb("dinv", [P, 2, T])
        xhat = sb("xhat", [P, 2, T, D])
        xhat_t = sb("xhat_t", [P, GT])
        adj_t = sb("adj_t", [P, T, P])
        feats = sb("feats", [P, T, D])
        agg = sb("agg", [P, T, D])
        rows = sb("rows", [P, SLOTS, T, ROW])
        bn2 = sb("bn2", [P, T, 6])
        mean2 = sb("mean2", [P, T])
        var2 = sb("var2", [P, T])
        x2hat = sb("x2hat", [P, T, D])
        x2hat_t = sb("x2hat_t", [P, 2, GT])
        hidden = sb("hidden", [P, 2, HC, GT])
        logits_t = sb("logits_t", [P, GT])
        top = sb("top", [P, T])
        below = sb("below", [P, T, E])
        cand = sb("cand", [P, T, E])
        best = sb("best", [P, T])
        chosen = sb("chosen", [P, T, E], BF16)
        tanh_half = sb("tanh_half", [P, T, E])
        soft = sb("soft", [P, T, E])
        soft_r = sb("soft_r", [P, T, E])
        soft_sum = sb("soft_sum", [P, T])
        denom = sb("denom", [P, T])
        base = sb("base", [P, E])
        place = sb("place", [P, T, E])
        place_own = sb("place_own", [P, T, E])
        place_sum = sb("place_sum", [P, T])
        index = sb("index", [P, 2, T], I32)

        region_i = sb("region_i", [P, E], I32)
        region0 = sb("region0", [P, E])
        count_f = sb("count_f", [1, E])
        count_i = sb("count_i", [1, E], I32)
        ntile_i = sb("ntile_i", [1, E], I32)
        ntile_f = sb("ntile_f", [1, E])
        upto = sb("upto", [1, E, E])
        ntile_upto = sb("ntile_upto", [1, E, E])
        last_tile = sb("last_tile", [1, E])
        jump = sb("jump", [1, E])
        tile_no_i = sb("tile_no_i", [1, TILES], I32)
        tile_no = sb("tile_no", [1, TILES])
        passed = sb("passed", [1, TILES, E])
        jumped = sb("jumped", [1, TILES, E])
        tile_e = sb("tile_e", [1, TILES])
        tile_r = sb("tile_r", [1, TILES])
        tile_r2 = sb("tile_r2", [1, TILES])
        tile_col = sb("tile_col", [1, TILES], I32)
        tile_row = sb("tile_row", [1, TILES], I32)
        fill_row = sb("fill_row", [1, E], I32)
        filler = sb("filler", [P, ROW])

        rows_b = sb("rows_b", [P, SLOTS, T, ROW])
        yhat = sb("yhat", [P, T, D])
        yhat_hi = sb("yhat_hi", [P, 2, GT], F32R)
        yhat_lo = sb("yhat_lo", [P, 2, GT], F32R)
        result = sb("result", [P, SLOTS, T, D])
        token = sb("token", [P, SLOTS, T], I32)

        ps_x = bank("ps_x")
        ps_a = bank("ps_a")
        ps_f = bank("ps_f")
        ps_u = bank("ps_u")
        ps_h = [bank("ps_h0"), bank("ps_h1")]
        ps_g = bank("ps_g")
        ps_r = bank("ps_r")
        logit_ps = ps_r[:, 0:T * E].rearrange("p (t e) -> p t e", t=T)
        rank_ps = ps_r[:, 64:64 + (T + 1) * E].rearrange("p (t e) -> p t e", t=T + 1)
        ps_y = [ps_a, ps_f, ps_u, ps_g]

        gnn_in = sem("gnn_in")
        ffn_in = sem("ffn_in")
        experts_in = sem("experts_in")
        const_pool = sem("const_pool")
        const_dve = sem("const_dve")
        wt_ps = sem("wt_ps")
        wt_sb = sem("wt_sb")
        bd_in = sem("bd_in")
        v1_setup = sem("v1_setup")
        x_load = [sem(f"x_load{s}") for s in range(SLOTS)]
        a_load = [sem(f"a_load{s}") for s in range(SLOTS)]
        v1_step = sem("v1_step")
        stat1 = sem("stat1")
        pow1 = sem("pow1")
        dinv_ok = sem("dinv_ok")
        xhat_ok = sem("xhat_ok")
        xt_ps = sem("xt_ps")
        xt_sb = sem("xt_sb")
        at_ps = sem("at_ps")
        at_sb = sem("at_sb")
        f_ps = sem("f_ps")
        f_sb = sem("f_sb")
        u_ps = sem("u_ps")
        agg_ok = sem("agg_ok")
        x1_ok = sem("x1_ok")
        v4_step = sem("v4_step")
        stat2 = sem("stat2")
        pow2 = sem("pow2")
        v5_step = sem("v5_step")
        x2hat_ok = sem("x2hat_ok")
        x2t_ps = sem("x2t_ps")
        x2t_sb = sem("x2t_sb")
        h_ps = sem("h_ps")
        h_sb = sem("h_sb")
        g_ps = sem("g_ps")
        lt_sb = sem("lt_sb")
        l_ps = sem("l_ps")
        v6_step = sem("v6_step")
        chosen_ok = sem("chosen_ok")
        tanh_ok = sem("tanh_ok")
        rank_ok = sem("rank_ok")
        v7_step = sem("v7_step")
        paced = sem("paced")
        row_ok = sem("row_ok")
        scattered = [sem(f"scattered{s}") for s in range(SLOTS)]
        tab_step = sem("tab_step")
        tab_ok = sem("tab_ok")
        fill_ok = sem("fill_ok")
        fill_in = sem("fill_in")
        b_load = [sem(f"b_load{s}") for s in range(SLOTS)]
        yhat_ok = sem("yhat_ok")
        yt_ps = sem("yt_ps")
        yhi_sb = sem("yhi_sb")
        ylo_sb = sem("ylo_sb")
        bh_ps = sem("bh_ps")
        bh_sb = sem("bh_sb")
        y_ps = sem("y_ps")
        res_ok = sem("res_ok")
        stored = [sem(f"stored{s}") for s in range(SLOTS)]

        block = ctx.enter_context(nc.Block())

        def after(eng, s, n):
            if not (isinstance(n, int) and n <= 0):
                eng.wait_ge(s, n)

        out_rows = out.rearrange("b n c -> (b n) c")
        x_view = x.rearrange("(g t) p f -> g p t f", t=T)
        adj_view = adj.rearrange("(g t) p m -> g p t m", t=T)

        A_FIRST, A_LOOP, A_END = -2, 5, GROUPS - 3

        def phase_a(eng, body):
            for c in range(A_FIRST, A_LOOP):
                body(0, c)
            with eng.Fori(0, (A_END - A_LOOP) // 4) as k:
                for j in range(4):
                    body(k, A_LOOP + j)
            for c in range(A_END, GROUPS + 4):
                body(0, c)

        def group(k, c):
            if isinstance(k, int) and not 0 <= c < GROUPS:
                return None
            return Step(k, c)

        B_LOOP, B_END = 5, QUADS - 5
        assert (A_END - A_LOOP) % 4 == 0 and (B_END - B_LOOP) % 4 == 0

        def phase_b(eng, body):
            for c in range(-1, B_LOOP):
                body(0, c)
            with eng.Fori(0, (B_END - B_LOOP) // 4) as k:
                for j in range(4):
                    body(k, B_LOOP + j)
            for c in range(B_END, QUADS + 1):
                body(0, c)

        def quad(k, c):
            if isinstance(k, int) and not 0 <= c < QUADS:
                return None
            return Step(k, c)

    
        def fill(eng, experts):
            eng.wait_ge(fill_ok, 1)
            for e in experts:
                r = eng.value_load(fill_row[0:1, e:e + 1], min_val=0, max_val=E * REGION - P)
                eng.dma_start(table[bass.ds(r, P)], filler[:]).then_inc(fill_in, 16)

        @block.sync
        def _(sp):
            def load_group(g):
                after(sp, x1_ok, g.n - 3)
                sp.dma_start(x_in[:, g.slot4], x_view[bass.ds(g.n, 1)].rearrange("a p t f -> (a p) t f")
                             ).then_inc(x_load[g.slot4], 16)
                after(sp, at_ps, g.n - 3)
                after(sp, stat1, g.n - 3)
                sp.dma_start(adj_in[:, g.slot4], adj_view[bass.ds(g.n, 1)].rearrange("a p t f -> (a p) t f")
                             ).then_inc(a_load[g.slot4], 16)

            load_group(Step(0, 0))
            load_group(Step(0, 1))

            def body(k, c):
                g = group(k, c + 1)
                if g and not (g.fixed and g.n < 2):
                    load_group(g)

            phase_a(sp, body)

            sp.wait_ge(v1_setup, 7)
            for part in range(3):
                sp.dma_start(bd3[part:part + 1], bd_part[:, part]).then_inc(bd_in, 16)
            sp.dma_start(table[E * REGION:E * REGION + P], filler[:]).then_inc(fill_in, 16)
            fill(sp, range(E // 2))
            sp.wait_ge(fill_in, 16 * (1 + E))
            for s in range(SLOTS):
                sp.wait_ge(scattered[s], 16 * T * (GROUPS // SLOTS))
            sp.wait_ge(tab_ok, 1)

            def load_quad(q):
                after(sp, res_ok, q.n - 3)
                for t in range(T):
                    r = sp.value_load(tile_row[0:1, bass.ds(T * q.n + t, 1)], min_val=0, max_val=E * REGION)
                    sp.dma_start(rows_b[:, q.slot4, t], table[bass.ds(r, P)]).then_inc(b_load[q.slot4], 16)

            for n in range(SLOTS):
                load_quad(Step(0, n))

            def body(k, c):
                q = quad(k, c + SLOTS - 1)
                if q and not (q.fixed and q.n < SLOTS):
                    load_quad(q)

            phase_b(sp, body)

        @block.gpsimd
        def _(pool):
            pool.memset(bg_col[:], 0.0).then_inc(const_pool, 1)
            pool.memset(minus_half[:], -0.5)
            pool.memset(pace[:], 0.0)
            pool.memset(ident[:], 0.0)
            pool.memset(gate_sum[:], 0.0)
            pool.memset(earlier[:], 1.0)
            pool.memset(ones[:], 1.0)
            pool.memset(wg_sb[:], 0.0)
            pool.memset(upto[:], 1.0)
            pool.memset(filler[:], 0.0)
            pool.iota(region_i[:], [[REGION // P, E]], base=0, channel_multiplier=0)
            pool.iota(tile_no_i[:], [[1, TILES]], base=0, channel_multiplier=0)
            pool.iota(seed_tok[:], [[P, T]], base=0, channel_multiplier=1)
            pool.iota(first_wins[:], [[0, T], [-1, E]], base=E, channel_multiplier=0,
                      allow_small_or_imprecise_dtypes=True).then_inc(const_pool, 1)
            pool.wait_ge(const_pool, 2)
            pool.affine_select(out=ident[:], in_=ident[:], compare_op=ALU.not_equal, fill=1.0, base=0,
                               pattern=[[-1, P]], channel_multiplier=1)
            pool.affine_select(out=earlier[:], in_=earlier[:], compare_op=ALU.is_gt, fill=0.0, base=0,
                               pattern=[[1, P]], channel_multiplier=-1)
            pool.affine_select(out=upto[:], in_=upto[:], compare_op=ALU.is_ge, fill=0.0, base=0,
                               pattern=[[1, E], [-1, E]], channel_multiplier=0)
            for c in range(HC):
                if c:
                    pool.wait_ge(const_pool, 2 + c)
                pool.affine_select(out=gate_sum[:], in_=gate_sum[:], compare_op=ALU.not_equal, fill=1.0,
                                   base=-32 * c, pattern=[[-1, E]], channel_multiplier=1
                                   ).then_inc(const_pool, 1)
            pool.wait_ge(ffn_in, 16 * 4)
            pool.tensor_copy(wg_sb[:, :, 0:E], wg_in[:]).then_inc(const_pool, 1)

            def powers1(g):
                pool.wait_ge(stat1, g.n + 1)
                after(pool, xhat_ok, g.n)
                pool.tensor_tensor(pow_out[:], pow_in[:], minus_half[:], ALU.pow).then_inc(pow1, 1)

            def powers2(g):
                pool.wait_ge(stat2, g.n + 1)
                pool.tensor_tensor(rows[:, g.slot4, :, C_RSTD], var2[:], minus_half[:, 0:T], ALU.pow
                                   ).then_inc(pow2, 1)

            def scatter(g, tiles):
                if 0 in tiles:
                    pool.wait_ge(row_ok, g.n + 1)
                    pool.tensor_tensor(pace_out[:, g.slot4:g.slot4 + 1], pace[:], pace[:], ALU.add).then_inc(paced, 1)
                for t in tiles:
                    pool.indirect_dma_start(table, bass.IndirectOffsetOnAxis(ap=index[:, g.slot2, t:t + 1], axis=0),
                                            rows[:, g.slot4, t], None).then_inc(scattered[g.slot4], 16)

            def body(k, c):
                if g := group(k, c - 1):
                    powers2(g)
                if g := group(k, c - 4):
                    scatter(g, (2, 3))
                if g := group(k, c + 2):
                    powers1(g)
                if g := group(k, c - 3):
                    scatter(g, (0, 1))

            phase_a(pool, body)

            last_token = pool.to_reg(TOKENS - 1)

            def store(q):
                pool.wait_ge(res_ok, q.n + 1)
                after(pool, paced, GROUPS + q.n)
                pool.tensor_tensor(pace_out[:, q.slot4:q.slot4 + 1], pace[:], pace[:], ALU.add).then_inc(paced, 1)
                for t in range(T):
                    pool.indirect_dma_start(
                        out_rows, bass.IndirectOffsetOnAxis(
                            ap=token[:, q.slot4, t:t + 1], axis=0),
                        result[:, q.slot4, t], None, bounds_check=last_token, oob_is_err=False,
                    ).then_inc(stored[q.slot4], 16)

            def body(k, c):
                if q := quad(k, c - 1):
                    store(q)

            phase_b(pool, body)
            for s in range(SLOTS):
                pool.wait_ge(stored[s], 16 * T * len(range(s, QUADS, SLOTS)))

        @block.tensor
        def _(pe):
            pe.wait_ge(const_pool, 2 + HC)
            pe.wait_ge(gnn_in, 16 * 2)
            pe.transpose(ps_f[:, 0:P], gnn_w_sb[:], ident[:]).then_inc(wt_ps, 1)
            pe.wait_ge(wt_sb, 1)

            def adj_transposes(g):
                pe.wait_ge(a_load[g.slot4], 16 * (g.nth4 + 1))
                after(pe, at_sb, g.n)
                for t in range(T):
                    last = pe.transpose(ps_a[:, t * P:(t + 1) * P], adj_in[:, g.slot4, t], ident[:])
                last.then_inc(at_ps, 1)

            def xhat_transposes(g):
                pe.wait_ge(xhat_ok, g.n + 1)
                after(pe, xt_sb, g.n)
                after(pe, x2t_sb, g.n - 1)
                for t in range(T):
                    last = pe.transpose(ps_x[:, t * P:(t + 1) * P], xhat[:, g.slot2, t], ident[:])
                last.then_inc(xt_ps, 1)

            def features(g):
                pe.wait_ge(xt_sb, g.n + 1)
                after(pe, f_sb, g.n)
                for t in range(T):
                    last = pe.matmul(ps_f[:, t * D:(t + 1) * D], xhat_t[:, t * P:(t + 1) * P], gnn_wt[:],
                                     start=True, stop=True)
                last.then_inc(f_ps, 1)

            def aggregate(g):
                pe.wait_ge(f_sb, g.n + 1)
                pe.wait_ge(at_sb, g.n + 1)
                after(pe, agg_ok, g.n)
                for t in range(T):
                    last = pe.matmul(ps_u[:, t * D:(t + 1) * D], adj_t[:, t], feats[:, t], start=True, stop=True)
                last.then_inc(u_ps, 1)

            def x2_transposes(g):
                pe.wait_ge(x2hat_ok, g.n + 1)
                pe.wait_ge(xt_sb, g.n + 1)
                if not (g.fixed and g.n == GROUPS - 1):
                    pe.wait_ge(xt_sb, g.n + 2)
                after(pe, x2t_sb, g.n)
                for t in range(T):
                    last = pe.transpose(ps_x[:, t * P:(t + 1) * P], x2hat[:, t], ident[:])
                last.then_inc(x2t_ps, 1)

            def hidden_chunk(g, c):
                if c == 0:
                    pe.wait_ge(x2t_sb, g.n + 1)
                    if g.fixed and g.n == 0:
                        pe.wait_ge(ffn_in, 16 * 4)
                after(pe, h_sb, HC * g.n + c - 1)
                pe.matmul(ps_h[c % 2][:], w1_sb[:, c * P:(c + 1) * P], x2hat_t[:, g.slot2], start=True, stop=True
                          ).then_inc(h_ps, 1)

            def gate(g):
                pe.wait_ge(h_sb, HC * (g.n + 1))
                if g.fixed and g.n == 0:
                    pe.wait_ge(const_pool, 3 + HC)
                after(pe, lt_sb, g.n)
                for c in range(HC):
                    last = pe.matmul(ps_g[32 * c:32 * c + 32], wg_sb[:, c], hidden[:, 0, c], start=True, stop=True)
                last.then_inc(g_ps, 1)

            def logits(g):
                pe.wait_ge(lt_sb, g.n + 1)
                after(pe, row_ok, g.n)
                for t in range(T):
                    last = pe.matmul(logit_ps[:, t], logits_t[:, t * P:(t + 1) * P], gate_sum[:], start=True, stop=True)
                last.then_inc(l_ps, 1)

            def ranks(g):
                pe.wait_ge(chosen_ok, g.n + 1)
                pe.matmul(rank_ps[:, 0:T], earlier[:], chosen[:], start=True, stop=False, skip_group_check=True)
                for t in range(T):
                    n = T - t
                    last = pe.matmul(rank_ps[:, t + 1:T + 1], ones[:],
                                     chosen[:, t:t + 1].to_broadcast([P, n, E]), start=False, stop=(t == T - 1),
                                     skip_group_check=True)
                last.then_inc(rank_ok, 1)

            def body(k, c):
                cur, two, three, one = group(k, c), group(k, c - 2), group(k, c - 3), group(k, c - 1)
                if cur:
                    xhat_transposes(cur)
                    adj_transposes(cur)
                if three:
                    gate(three)
                if cur:
                    features(cur)
                if three:
                    logits(three)
                if two:
                    hidden_chunk(two, 0)
                if cur:
                    aggregate(cur)
                if three:
                    ranks(three)
                if two:
                    hidden_chunk(two, 1)
                if one:
                    x2_transposes(one)
                if two:
                    hidden_chunk(two, 2)
                    hidden_chunk(two, 3)

            phase_a(pe, body)

            pe.wait_ge(bd_in, 48)
            pe.wait_ge(experts_in, 16 * (1 + HC))
            pe.wait_ge(const_dve, 1)
            pe.wait_ge(tab_ok, 1)

            def yhat_transposes(q):
                pe.wait_ge(yhat_ok, q.n + 1)
                after(pe, ylo_sb, q.n)
                for t in range(T):
                    last = pe.transpose(ps_x[:, t * P:(t + 1) * P], yhat[:, t], ident[:])
                last.then_inc(yt_ps, 1)

            def hidden_b(q, c):
                if c == 0:
                    pe.wait_ge(yhi_sb, q.n + 1)
                    pe.wait_ge(ylo_sb, q.n + 1)
                after(pe, bh_sb, HC * q.n + c - 1)
                w = slice(c * P, (c + 1) * P)
                pe.matmul(ps_h[c % 2][:], w1_hi[:, w], yhat_hi[:, q.slot2], start=True, stop=False)
                pe.matmul(ps_h[c % 2][:], w1_hi[:, w], yhat_lo[:, q.slot2], start=False, stop=False)
                pe.matmul(ps_h[c % 2][:], w1_lo[:, w], yhat_hi[:, q.slot2], start=False, stop=True
                          ).then_inc(bh_ps, 1)

            def expert(q, t):
                col = pe.value_load(tile_col[0:1, bass.ds(T * q.n + t, 1)], min_val=0, max_val=(E - 1) * D)
                if t == 0:
                    pe.wait_ge(bh_sb, HC * (q.n + 1))
                after(pe, res_ok, q.n)
                pe.matmul(ps_y[t][:, 0:D], ones[0:3, :], bd3[:, bass.ds(col, D)], start=True, stop=False)
                for c in range(HC):
                    last = pe.matmul(ps_y[t][:, 0:D], hidden[:, q.slot2, c, t * P:(t + 1) * P],
                                     wd_sb[:, c, bass.ds(col, D)], start=False, stop=(c == HC - 1))
                last.then_inc(y_ps, 1)

            def body(k, c):
                prev, cur, nxt = quad(k, c - 1), quad(k, c), quad(k, c + 1)
                if cur:
                    hidden_b(cur, 0)
                if nxt:
                    yhat_transposes(nxt)
                if cur:
                    hidden_b(cur, 1)
                if prev:
                    expert(prev, 0)
                    expert(prev, 1)
                if cur:
                    hidden_b(cur, 2)
                if prev:
                    expert(prev, 2)
                    expert(prev, 3)
                if cur:
                    hidden_b(cur, 3)

            phase_b(pe, body)

        @block.scalar
        def _(act):
            act.dma_start(gnn_w_sb[:], gnn_w).then_inc(gnn_in, 16)
            act.dma_start(gnn_b_all[:], gnn_b.rearrange("(a b f) -> a b f", a=1, b=1).to_broadcast([P, T, D])
                          ).then_inc(gnn_in, 16)
            act.dma_start(w1_sb[:], w1).then_inc(ffn_in, 16)
            act.dma_start(b1_col[:], b1.rearrange("(c p) -> p c", p=P), allow_slow_non_contiguous=True
                          ).then_inc(ffn_in, 16)
            act.dma_start(wg_in[:], wg.rearrange("(c p) e -> p c e", p=P)).then_inc(ffn_in, 16)
            act.wait_ge(const_pool, 1)
            act.dma_start(bg_col[0:E], bg.rearrange("(e a) -> e a", a=1)).then_inc(ffn_in, 16)
            act.dma_start(bd_row[:], bd.rearrange("(a e) c -> a (e c)", a=1)).then_inc(experts_in, 16)
            for c in range(HC):
                act.dma_start(wd_sb[:, c].rearrange("p (e o) -> p e o", e=E),
                              wd[:, c * P:(c + 1) * P].rearrange("e p o -> p e o")).then_inc(experts_in, 16)

            def adj_copy(g):
                act.wait_ge(at_ps, g.n + 1)
                act.wait_ge(dinv_ok, g.n + 1)
                after(act, u_ps, g.n)
                for t in range(T):
                    last = act.activation(adj_t[:, t], ps_a[:, t * P:(t + 1) * P], ACT.Copy,
                                          scale=dinv[:, g.slot2, t:t + 1])
                last.then_inc(at_sb, 1)

            def xhat_copy(g):
                act.wait_ge(xt_ps, g.n + 1)
                after(act, f_ps, g.n)
                act.copy(xhat_t[:], ps_x[:]).then_inc(xt_sb, 1)

            def relu(g):
                act.wait_ge(u_ps, g.n + 1)
                after(act, x1_ok, g.n)
                for t in range(T):
                    last = act.activation(agg[:, t], ps_u[:, t * D:(t + 1) * D], ACT.Relu,
                                          scale=dinv[:, g.slot2, t:t + 1])
                last.then_inc(agg_ok, 1)

            def x2_copy(g):
                act.wait_ge(x2t_ps, g.n + 1)
                after(act, h_ps, HC * (g.n - 1))
                act.copy(x2hat_t[:, g.slot2], ps_x[:]).then_inc(x2t_sb, 1)

            def gelu(g, c):
                act.wait_ge(h_ps, HC * g.n + c + 1)
                if g.fixed and g.n == 0 and c == 0:
                    act.wait_ge(ffn_in, 16 * 4)
                after(act, g_ps, g.n)
                act.activation(hidden[:, 0, c], ps_h[c % 2][:], ACT.Gelu, bias=b1_col[:, c:c + 1]).then_inc(h_sb, 1)

            def logits_copy(g):
                act.wait_ge(g_ps, g.n + 1)
                after(act, l_ps, g.n)
                act.activation(logits_t[:], ps_g[:], ACT.Identity, bias=bg_col[:, 0:1]).then_inc(lt_sb, 1)

            def tanh(g):
                act.wait_ge(v6_step, 4 * g.n + 2)
                after(act, row_ok, g.n)
                act.activation(tanh_half[:], below[:], ACT.Tanh, scale=0.5).then_inc(tanh_ok, 1)


            def body(k, c):
                cur, two, three, one = group(k, c), group(k, c - 2), group(k, c - 3), group(k, c - 1)
                if cur:
                    xhat_copy(cur)
                    adj_copy(cur)
                if three:
                    logits_copy(three)
                if two:
                    gelu(two, 0)
                if cur:
                    relu(cur)
                if three:
                    tanh(three)
                if two:
                    gelu(two, 1)
                if one:
                    x2_copy(one)
                if two:
                    gelu(two, 2)
                    gelu(two, 3)

            phase_a(act, body)

            fill(act, range(E // 2, E))

            def yhat_copy(q):
                act.wait_ge(yt_ps, q.n + 1)
                after(act, bh_ps, HC * (q.n - 1))
                act.copy(yhat_hi[:, q.slot2], ps_x[:]).then_inc(yhi_sb, 1)

            def gelu_b(q, c):
                act.wait_ge(bh_ps, HC * q.n + c + 1)
                after(act, y_ps, T * (q.n - 1))
                act.activation(hidden[:, q.slot2, c], ps_h[c % 2][:], ACT.Gelu, bias=b1_col[:, c:c + 1]
                               ).then_inc(bh_sb, 1)

            def body(k, c):
                cur, nxt = quad(k, c), quad(k, c + 1)
                if cur:
                    gelu_b(cur, 0)
                if nxt:
                    yhat_copy(nxt)
                if cur:
                    gelu_b(cur, 1)
                    gelu_b(cur, 2)
                    gelu_b(cur, 3)

            phase_b(act, body)

        @block.vector
        def _(dve):
            dve.wait_ge(const_pool, 2)
            dve.tensor_copy(tok_f[:], seed_tok[:])
            dve.tensor_copy(tile_no[:], tile_no_i[:])
            dve.tensor_scalar(base[:], region_i[:], float(P), None, ALU.mult)
            dve.tensor_scalar(region0[:], region_i[:], float(P), None, ALU.mult).then_inc(v1_setup, 1)
            dve.wait_ge(v1_setup, 1)
            dve.tensor_scalar(filler[:, C_TOK:C_TOK + 1].bitcast(I32), base[:, 0:1], 0.0, float(TOKENS),
                              ALU.mult, ALU.add).then_inc(v1_setup, 1)
            dve.wait_ge(wt_ps, 1)
            dve.tensor_copy(gnn_wt[:], ps_f[:, 0:P]).then_inc(wt_sb, 1)

            def split_weights():
                dve.wait_ge(ffn_in, 16 * 4)
                dve.wait_ge(experts_in, 16 * (1 + HC))
                dve.tensor_copy(w1_hi[:], w1_sb[:])
                dve.tensor_copy(bd_part[:, 0], bd_row[:]).then_inc(v1_setup, 1)
                dve.wait_ge(v1_setup, 3)
                dve.tensor_tensor(w1_lo[:], w1_sb[:], w1_hi[:].bitcast(F32), ALU.subtract).then_inc(const_dve, 1)
                dve.tensor_tensor(bd_rest[:], bd_row[:], bd_part[:, 0], ALU.subtract).then_inc(v1_setup, 1)
                dve.wait_ge(v1_setup, 4)
                dve.tensor_copy(bd_part[:, 1], bd_rest[:]).then_inc(v1_setup, 1)
                dve.wait_ge(v1_setup, 5)
                dve.tensor_tensor(bd_row[:], bd_rest[:], bd_part[:, 1], ALU.subtract).then_inc(v1_setup, 1)
                dve.wait_ge(v1_setup, 6)
                dve.tensor_copy(bd_part[:, 2], bd_row[:]).then_inc(v1_setup, 1)

            def moments(bn, mean, step, done):
                even, odd = bn[:, :, 0:3], bn[:, :, 3:6]
                dve.tensor_tensor(m_sum[:], even[:, :, 1], odd[:, :, 1], ALU.add)
                dve.tensor_tensor(m_diff[:], even[:, :, 1], odd[:, :, 1], ALU.subtract)
                dve.tensor_tensor(m_sq[:], even[:, :, 2], odd[:, :, 2], ALU.add).then_inc(step, 1)
                dve.wait_ge(step, done + 1)
                dve.tensor_scalar(mean[:], m_sum[:], 0.5, None, ALU.mult)
                dve.scalar_tensor_tensor(m_between[:], m_diff[:], 0.25, m_diff[:], ALU.mult, ALU.mult)
                dve.tensor_scalar(m_within[:], m_sq[:], 1.0 / D, EPS, ALU.mult, ALU.add).then_inc(step, 1)

            def statistics1(g):
                dve.wait_ge(x_load[g.slot4], 16 * (g.nth4 + 1))
                for t in range(T):
                    last = dve.bn_stats(bn1[:, t], x_in[:, g.slot4, t])
                last.then_inc(v1_step, 1)
                dve.wait_ge(a_load[g.slot4], 16 * (g.nth4 + 1))
                after(dve, dinv_ok, g.n)
                dve.tensor_reduce(deg[:], adj_in[:, g.slot4], AX_X, ALU.add).then_inc(v1_step, 1)
                dve.wait_ge(v1_step, 4 * g.n + 1)
                after(dve, xhat_ok, g.n)
                moments(bn1, mean1, v1_step, 4 * g.n + 2)
                after(dve, pow1, g.n)
                dve.scalar_tensor_tensor(pow_in[:, 0:T], deg[:], 0.0, deg[:], ALU.is_equal, ALU.add)
                dve.wait_ge(v1_step, 4 * g.n + 4)
                dve.tensor_tensor(pow_in[:, T:2 * T], m_within[:], m_between[:], ALU.add).then_inc(stat1, 1)

            def normalize1(g):
                dve.wait_ge(pow1, g.n + 1)
                after(dve, agg_ok, g.n - 1)
                after(dve, at_sb, g.n - 1)
                dve.scalar_tensor_tensor(dinv[:, g.slot2], deg[:], 0.0, pow_out[:, 0:T], ALU.not_equal, ALU.mult
                                         ).then_inc(dinv_ok, 1)
                after(dve, xt_ps, g.n - 1)
                for t in range(T):
                    last = dve.tensor_scalar(xhat[:, g.slot2, t], x_in[:, g.slot4, t], mean1[:, t:t + 1],
                                             pow_out[:, T + t:T + t + 1], ALU.subtract, ALU.mult)
                last.then_inc(xhat_ok, 1)

            def add_bias(g):
                dve.wait_ge(f_ps, g.n + 1)
                after(dve, u_ps, g.n)
                dve.tensor_tensor(feats[:], ps_f[:].rearrange("p (t d) -> p t d", t=T), gnn_b_all[:], ALU.add
                                  ).then_inc(f_sb, 1)

            def residual(g):
                dve.wait_ge(agg_ok, g.n + 1)
                after(dve, scattered[g.slot4], 16 * T * g.nth4)
                dve.tensor_tensor(rows[:, g.slot4, :, 0:D], agg[:], x_in[:, g.slot4], ALU.add).then_inc(x1_ok, 1)
                dve.wait_ge(x1_ok, g.n + 1)
                for t in range(T):
                    last = dve.bn_stats(bn2[:, t], rows[:, g.slot4, t, 0:D])
                last.then_inc(v4_step, 1)
                dve.wait_ge(v4_step, 3 * g.n + 1)
                after(dve, x2hat_ok, g.n)
                moments(bn2, mean2, v4_step, 3 * g.n + 1)
                dve.wait_ge(v4_step, 3 * g.n + 3)
                after(dve, pow2, g.n)
                dve.tensor_tensor(var2[:], m_within[:], m_between[:], ALU.add).then_inc(stat2, 1)

            def normalize2(g):
                dve.wait_ge(pow2, g.n + 1)
                after(dve, x2t_ps, g.n)
                rstd = rows[:, g.slot4, :, C_RSTD]
                dve.scalar_tensor_tensor(rows[:, g.slot4, :, C_NMR], mean2[:], -1.0, rstd, ALU.mult, ALU.mult
                                         ).then_inc(v5_step, 1)
                for t in range(T):
                    last = dve.tensor_scalar(x2hat[:, t], rows[:, g.slot4, t, 0:D], mean2[:, t:t + 1],
                                             rows[:, g.slot4, t, C_RSTD:C_RSTD + 1], ALU.subtract, ALU.mult)
                last.then_inc(x2hat_ok, 1)

            def choose(g):
                dve.wait_ge(l_ps, g.n + 1)
                dve.tensor_reduce(top[:], logit_ps, AX_X, ALU.max).then_inc(v6_step, 1)
                dve.wait_ge(v6_step, 4 * g.n + 1)
                after(dve, tanh_ok, g.n)
                dve.tensor_tensor(below[:], logit_ps, top[:].rearrange("p (t a) -> p t a", a=1).to_broadcast([P, T, E]),
                                  ALU.subtract).then_inc(v6_step, 1)
                dve.wait_ge(v6_step, 4 * g.n + 2)
                dve.scalar_tensor_tensor(cand[:].rearrange("p t e -> p (t e)"), below[:].rearrange("p t e -> p (t e)"),
                                         0.0, first_wins[:].rearrange("p t e -> p (t e)"), ALU.is_equal, ALU.mult
                                         ).then_inc(v6_step, 1)
                dve.wait_ge(v6_step, 4 * g.n + 3)
                dve.tensor_reduce(best[:], cand[:], AX_X, ALU.max).then_inc(v6_step, 1)
                dve.wait_ge(v6_step, 4 * g.n + 4)
                dve.tensor_tensor(chosen[:], cand[:], best[:].rearrange("p (t a) -> p t a", a=1).to_broadcast([P, T, E]),
                                  ALU.is_equal).then_inc(chosen_ok, 1)

            def finish_rows(g):
                dve.wait_ge(tanh_ok, g.n + 1)
                dve.tensor_scalar(soft[:], tanh_half[:], -1.0, 1.0, ALU.mult, ALU.add).then_inc(v7_step, 1)
                dve.wait_ge(rank_ok, g.n + 1)
                dve.tensor_tensor(place[:], rank_ps[:, 0:T], base[:].rearrange("p (a e) -> p a e", a=1).to_broadcast(
                    [P, T, E]), ALU.add).then_inc(v7_step, 1)
                dve.wait_ge(v7_step, 8 * g.n + 1)
                dve.reciprocal(soft_r[:], soft[:]).then_inc(v7_step, 1)
                dve.wait_ge(v7_step, 8 * g.n + 2)
                dve.tensor_tensor(base[:], base[:], rank_ps[:, T], ALU.add).then_inc(v7_step, 1)
                dve.tensor_tensor(place_own[:], place[:], chosen[:], ALU.mult).then_inc(v7_step, 1)
                dve.wait_ge(v7_step, 8 * g.n + 3)
                dve.tensor_reduce(soft_sum[:], soft_r[:], AX_X, ALU.add).then_inc(v7_step, 1)
                dve.tensor_copy(rows[:, g.slot4, :, C_TOK].bitcast(I32), tok_f[:])
                dve.wait_ge(v7_step, 8 * g.n + 5)
                dve.tensor_reduce(place_sum[:], place_own[:], AX_X, ALU.add).then_inc(v7_step, 1)
                dve.wait_ge(v7_step, 8 * g.n + 6)
                dve.tensor_scalar(denom[:], soft_sum[:], 2.0, -float(E), ALU.mult, ALU.add).then_inc(v7_step, 1)
                dve.wait_ge(v7_step, 8 * g.n + 7)
                after(dve, scattered[(g.slot4 + 2) % 4], 16 * T * g.uses_back2)
                dve.tensor_copy(index[:, g.slot2], place_sum[:])
                dve.wait_ge(v7_step, 8 * g.n + 8)
                dve.tensor_scalar(tok_f[:], tok_f[:], float(GT), None, ALU.add)
                dve.reciprocal(rows[:, g.slot4, :, C_PROB], denom[:]).then_inc(row_ok, 1)

            def body(k, c):
                cur, nxt, far = group(k, c), group(k, c + 1), group(k, c + 2)
                three, one = group(k, c - 3), group(k, c - 1)
                if nxt:
                    normalize1(nxt)
                if cur:
                    add_bias(cur)
                if three:
                    choose(three)
                if one:
                    normalize2(one)
                if far:
                    statistics1(far)
                if three:
                    finish_rows(three)
                if cur:
                    residual(cur)
                if isinstance(k, int) and c == 1:
                    split_weights()

            phase_a(dve, body)

            steps = [0]

            def link(ins):
                steps[0] += 1
                ins.then_inc(tab_step, 1)
                dve.wait_ge(tab_step, steps[0])

            dve.wait_ge(row_ok, GROUPS)
            dve.tensor_copy(fill_row[:], base[0:1, :]).then_inc(fill_ok, 1)
            link(dve.tensor_tensor(count_f[:], base[0:1, :], region0[0:1, :], ALU.subtract))
            link(dve.tensor_scalar(count_i[:], count_f[:], float(P - 1), None, ALU.add))
            link(dve.tensor_scalar(ntile_i[:], count_i[:], P.bit_length() - 1, None, ALU.logical_shift_right))
            link(dve.tensor_copy(ntile_f[:], ntile_i[:]))
            link(dve.tensor_tensor(ntile_upto[:], upto[:], ntile_f[:].rearrange("p (a e) -> p a e", a=1).to_broadcast(
                [1, E, E]), ALU.mult))
            link(dve.tensor_scalar(jump[:], ntile_f[:], -float(P), float(REGION), ALU.mult, ALU.add))
            link(dve.tensor_reduce(last_tile[:], ntile_upto[:], AX_X, ALU.add))
            link(dve.tensor_tensor(passed[:], tile_no[:].rearrange("p (j a) -> p j a", a=1).to_broadcast([1, TILES, E]),
                                   last_tile[:].rearrange("p (a e) -> p a e", a=1).to_broadcast([1, TILES, E]),
                                   ALU.is_ge))
            link(dve.tensor_tensor(jumped[:], passed[:], jump[:].rearrange("p (a e) -> p a e", a=1).to_broadcast(
                [1, TILES, E]), ALU.mult))
            link(dve.tensor_reduce(tile_e[:], passed[:], AX_X, ALU.add))
            link(dve.tensor_reduce(tile_r[:], jumped[:], AX_X, ALU.add))
            link(dve.scalar_tensor_tensor(tile_r2[:], tile_no[:], float(P), tile_r[:], ALU.mult, ALU.add))
            link(dve.tensor_scalar(tile_row[:], tile_r2[:], float(E * REGION), None, ALU.min))
            link(dve.tensor_scalar(tile_col[:], tile_e[:], float(E - 1), float(D), ALU.min, ALU.mult))
            dve.engine_nop().then_inc(tab_ok, 1)

            def normalize_b(q):
                dve.wait_ge(b_load[q.slot4], 16 * T * (q.nth4 + 1))
                after(dve, yt_ps, q.n)
                for t in range(T):
                    r = rows_b[:, q.slot4, t]
                    last = dve.tensor_scalar(yhat[:, t], r[:, 0:D], r[:, C_RSTD:C_RSTD + 1], r[:, C_NMR:C_NMR + 1],
                                             ALU.mult, ALU.add)
                last.then_inc(yhat_ok, 1)

            def low_part(q):
                dve.wait_ge(yhi_sb, q.n + 1)
                dve.tensor_tensor(yhat_lo[:, q.slot2], ps_x[:], yhat_hi[:, q.slot2].bitcast(F32), ALU.subtract
                                  ).then_inc(ylo_sb, 1)

            def results(q, t):
                dve.wait_ge(y_ps, T * q.n + t + 1)
                if t == 0:
                    after(dve, stored[q.slot4], 16 * T * q.nth4)
                    dve.tensor_copy(token[:, q.slot4], rows_b[:, q.slot4, :, C_TOK].bitcast(I32))
                r = rows_b[:, q.slot4, t]
                last = dve.scalar_tensor_tensor(result[:, q.slot4, t], ps_y[t][:, 0:D], r[:, C_PROB:C_PROB + 1],
                                                r[:, 0:D], ALU.mult, ALU.add)
                if t == T - 1:
                    last.then_inc(res_ok, 1)

            def body(k, c):
                prev, nxt, far = quad(k, c - 1), quad(k, c + 1), quad(k, c + 2)
                if nxt and nxt.fixed and nxt.n == 0:
                    normalize_b(nxt)
                if nxt:
                    low_part(nxt)
                if prev:
                    for t in range(T):
                        results(prev, t)
                if far:
                    normalize_b(far)

            phase_b(dve, body)


_INS = ["x", "adj", "L0_gnn_W", "L0_gnn_b", "L0_ffn_W1", "L0_ffn_b1", "L0_ffn_Wg", "L0_ffn_bg", "L0_ffn_Wd",
        "L0_ffn_bd"]


def kernel(**inputs):
    import numpy as _np
    import concourse.bacc as _bacc
    from concourse import mybir as _mybir
    from concourse.bass_utils import run_bass_kernel_spmd as _run

    nc = _bacc.Bacc("TRN2", target_bir_lowering=False, num_devices=1)
    arrays, args = {}, []
    for name in _INS:
        a = _np.ascontiguousarray(inputs[name])
        arrays[f"in_{name}_dram"] = a
        args.append(nc.dram_tensor(f"in_{name}_dram", a.shape, _mybir.dt.from_np(a.dtype), kind="ExternalInput").ap())
    result = nc.dram_tensor("out_0_dram", (GRAPHS, P, D), F32, kind="ExternalOutput").ap()
    moe_gnn_kernel(nc, *args, result)
    r = _run(nc, [arrays], core_ids=[0])
    return r.results[0]["out_0_dram"]
```

```python
from contextlib import ExitStack

import concourse.bass as bass
from concourse import mybir

ALU = mybir.AluOpType
ACT = mybir.ActivationFunctionType
AX_X = mybir.AxisListType.X
F32 = mybir.dt.float32
F32R = mybir.dt.float32r
BF16 = mybir.dt.bfloat16
I32 = mybir.dt.int32

P = 128
GRAPHS = 128
TOKENS = GRAPHS * P
D = 128
HID = 512
HC = HID // P
E = 8
T = 4
GROUPS = GRAPHS // T
GT = T * P
EPS = 1e-5
ROW = D + 3 + E
C_MEAN, C_RSTD, C_TOK, C_BELOW = D, D + 1, D + 2, D + 3
REGION = TOKENS + P
TILES = TOKENS // P + E
QUADS = TILES // T
COPIED_BIASES = 2
DVE_TILES = 3
UA, UB = 6, 6


class Step:

    def __init__(self, unroll, k, c):
        self.n = unroll * k + c
        self.slot, self.slot2, self.slot3 = c % unroll, c % 2, c % 3
        self.nth = k + c // unroll
        self.fixed = isinstance(k, int)


def moe_gnn_kernel(nc, x, adj, gnn_w, gnn_b, w1, b1, wg, bg, wd, bd, out):
    with ExitStack() as ctx:
        def sb(name, shape, dt=F32):
            return ctx.enter_context(nc.sbuf_tensor(name, shape, dt))

        def bank(name, shape=(P, 512), dt=F32):
            return ctx.enter_context(nc.psum_tensor(name, list(shape), dt))

        def sem(name):
            return ctx.enter_context(nc.semaphore(name))

        table = nc.dram_tensor("table", [E * REGION + P, ROW], F32).ap()

        ident = sb("ident", [P, P])
        earlier = sb("earlier", [P, P], BF16)
        ones = sb("ones", [P, P], BF16)
        first_wins = sb("first_wins", [P, T, E])
        seed_tok = sb("seed_tok", [P, T], I32)
        group_tokens = sb("group_tokens", [P, T])
        minus_half = sb("minus_half", [P, 2 * T])
        pace = sb("pace", [1, 1])
        gelu_warm = sb("gelu_warm", [1, 1])
        pace_out = sb("pace_out", [1, UB])
        gnn_w_sb = sb("gnn_w_sb", [P, D])
        gnn_wt = sb("gnn_wt", [P, D])
        gnn_b_row = sb("gnn_b_row", [1, D])
        gnn_b_rest = sb("gnn_b_rest", [1, 2, D])
        gnn_b_part = sb("gnn_b_part", [1, 3, T, D], BF16)
        gnn_b3 = sb("gnn_b3", [3, GT], BF16)
        w1_sb = sb("w1_sb", [P, HID])
        w1_hi = sb("w1_hi", [P, HID], F32R)
        w1_lo = sb("w1_lo", [P, HID], F32R)
        b1_col = sb("b1_col", [P, HC])
        wg_sb = sb("wg_sb", [P, HC, 32])
        wg_in = sb("wg_in", [P, HC, E])
        bg_col = sb("bg_col", [P, 1])
        wd_sb = sb("wd_sb", [P, HC, E * D])
        bd_all = sb("bd_all", [P, E * D])

        x_in = sb("x_in", [P, UA, T, D])
        adj_in = sb("adj_in", [P, UA, T, P])
        bn = sb("bn", [P, 2 * T, 6])
        m_sum = sb("m_sum", [P, 2 * T])
        m_diff = sb("m_diff", [P, 2 * T])
        m_sq = sb("m_sq", [P, 2 * T])
        m_between = sb("m_between", [P, 2 * T])
        m_within = sb("m_within", [P, 2 * T])
        mean1 = sb("mean1", [P, T])
        shift1 = sb("shift1", [P, T])
        deg = sb("deg", [P, 2, T])
        pow_in = sb("pow_in", [P, 3 * T])
        pow_out = sb("pow_out", [P, 2 * T])
        dinv = sb("dinv", [P, 2, T])
        xhat = sb("xhat", [P, T, D])
        xhat_t = sb("xhat_t", [P, GT])
        adj_t = sb("adj_t", [P, T, P])
        feats = sb("feats", [P, T, D])
        agg = sb("agg", [P, T, D])
        rows = sb("rows", [P, UA, T, ROW])
        x2hat = sb("x2hat", [P, T, D])
        x2hat_hi = sb("x2hat_hi", [P, 2, GT], F32R)
        x2hat_lo = sb("x2hat_lo", [P, 2, GT], F32R)
        hidden = sb("hidden", [P, 2, HC, GT])
        logits_t = sb("logits_t", [P, GT])
        logit = sb("logit", [P, T, E])
        top = sb("top", [P, T])
        cand = sb("cand", [P, T, E])
        best = sb("best", [P, T])
        chosen = sb("chosen", [P, T, E], BF16)
        base = sb("base", [P, E])
        place = sb("place", [P, T, E])
        place_own = sb("place_own", [P, T, E])
        index = sb("index", [P, UA, T], I32)

        region_i = sb("region_i", [P, E], I32)
        region0 = sb("region0", [P, E])
        count_f = sb("count_f", [T, E])
        count_i = sb("count_i", [T, E], I32)
        ntile_i = sb("ntile_i", [T, E], I32)
        ntile_f = sb("ntile_f", [T, E])
        upto = sb("upto", [T, E, E])
        ntile_upto = sb("ntile_upto", [T, E, E])
        last_tile = sb("last_tile", [T, E])
        jump = sb("jump", [T, E])
        tile_no_i = sb("tile_no_i", [T, QUADS], I32)
        tile_no = sb("tile_no", [T, QUADS])
        passed = sb("passed", [T, QUADS, E])
        jumped = sb("jumped", [T, QUADS, E])
        tile_e = sb("tile_e", [T, QUADS])
        tile_r = sb("tile_r", [T, QUADS])
        tile_r2 = sb("tile_r2", [T, QUADS])
        tile_col = sb("tile_col", [T, QUADS], I32)
        tile_row = sb("tile_row", [T, QUADS], I32)
        fill_row = sb("fill_row", [1, E], I32)
        filler = sb("filler", [P, ROW])

        rows_b = sb("rows_b", [P, UB, T, ROW])
        tanh_half = sb("tanh_half", [P, T, E])
        soft = sb("soft", [P, T, E])
        soft_r = sb("soft_r", [P, T, E])
        soft_sum = sb("soft_sum", [P, T])
        denom = sb("denom", [P, T])
        prob = sb("prob", [P, 2, T])
        biased = sb("biased", [P, 2, T, D])
        bias_copy = sb("bias_copy", [P, 2, T, D])
        yhat = sb("yhat", [P, T, D])
        yhat_hi = sb("yhat_hi", [P, 2, GT], F32R)
        yhat_lo = sb("yhat_lo", [P, 2, GT], F32R)
        result = sb("result", [P, UB, T, D])
        token = sb("token", [P, UB, T], I32)

        ps_x = bank("ps_x")
        ps_a = bank("ps_a")
        ps_f = bank("ps_f")
        ps_u = bank("ps_u")
        ps_h = [bank("ps_h0"), bank("ps_h1")]
        ps_g = bank("ps_g")
        ps_r = bank("ps_r")
        partial_ps = ps_r[:].rearrange("p (t c e) -> p t e c", t=T, c=HC)[:, :, 0:E]
        rank_ps = ps_r[:, 64:64 + (T + 1) * E].rearrange("p (t e) -> p t e", t=T + 1)
        ps_y = [ps_a, ps_f, ps_u, ps_g]

        gnn_in = sem("gnn_in")
        gnn_b_step = sem("gnn_b_step")
        gnn_b_in = sem("gnn_b_in")
        ffn_in = sem("ffn_in")
        experts_in = sem("experts_in")
        const_pool = sem("const_pool")
        const_dve = sem("const_dve")
        wt_ps = sem("wt_ps")
        wt_sb = sem("wt_sb")
        bd_in = sem("bd_in")
        v1_setup = sem("v1_setup")
        x_load = [sem(f"x_load{s}") for s in range(UA)]
        a_load = [sem(f"a_load{s}") for s in range(UA)]
        at_ps = sem("at_ps")
        at_sb = sem("at_sb")
        moment_step = sem("moment_step")
        stat = sem("stat")
        pow1 = sem("pow1")
        pow2 = sem("pow2")
        deg_ok = sem("deg_ok")
        dinv_ok = sem("dinv_ok")
        xhat_ok = sem("xhat_ok")
        xhat_act = sem("xhat_act")
        shift1_ok = sem("shift1_ok")
        xt_ps = sem("xt_ps")
        xt_sb = sem("xt_sb")
        f_ps = sem("f_ps")
        f_sb = sem("f_sb")
        u_ps = sem("u_ps")
        agg_ok = sem("agg_ok")
        x1_ok = sem("x1_ok")
        x2hat_ok = sem("x2hat_ok")
        x2t_ps = sem("x2t_ps")
        x2hi_sb = sem("x2hi_sb")
        x2lo_sb = sem("x2lo_sb")
        h_ps = sem("h_ps")
        h_sb = sem("h_sb")
        g_ps = sem("g_ps")
        lt_sb = sem("lt_sb")
        l_ps = sem("l_ps")
        choose_step = sem("choose_step")
        chosen_ok = sem("chosen_ok")
        rank_ok = sem("rank_ok")
        place_step = sem("place_step")
        row_ok = sem("row_ok")
        numbered = sem("numbered")
        scattered = [sem(f"scattered{s}") for s in range(UA)]
        tab_step = sem("tab_step")
        tab_ok = sem("tab_ok")
        fill_ok = sem("fill_ok")
        fill_in = sem("fill_in")
        b_load = [sem(f"b_load{s}") for s in range(UB)]
        tanh_ok = sem("tanh_ok")
        prob_step = sem("prob_step")
        prob_ok = sem("prob_ok")
        bias_ok = sem("bias_ok")
        biased_ok = sem("biased_ok")
        paced = sem("paced")
        yhat_ok = sem("yhat_ok")
        yt_ps = sem("yt_ps")
        yhi_sb = sem("yhi_sb")
        ylo_sb = sem("ylo_sb")
        bh_ps = sem("bh_ps")
        bh_sb = sem("bh_sb")
        y_ps = sem("y_ps")
        res_ok = sem("res_ok")
        stored = [sem(f"stored{s}") for s in range(UB)]

        block = ctx.enter_context(nc.Block())

        def after(eng, s, n):
            if not (isinstance(n, int) and n <= 0):
                eng.wait_ge(s, n)

        out_rows = out.rearrange("b n c -> (b n) c")
        x_view = x.rearrange("(g t) p f -> g p t f", t=T)
        adj_view = adj.rearrange("(g t) p m -> g p t m", t=T)

        A_FIRST, A_LOOP, A_END = -1, UA + 1, GROUPS - 7
        B_LOOP, B_END = UB + 1, QUADS - 9
        assert (A_END - A_LOOP) % UA == 0 and (B_END - B_LOOP) % UB == 0

        def phase_a(eng, body):
            for c in range(A_FIRST, A_LOOP):
                body(0, c)
            with eng.Fori(0, (A_END - A_LOOP) // UA) as k:
                for j in range(UA):
                    body(k, A_LOOP + j)
            for c in range(A_END, GROUPS + 4):
                body(0, c)

        def phase_b(eng, body):
            for c in range(-1, B_LOOP):
                body(0, c)
            with eng.Fori(0, (B_END - B_LOOP) // UB) as k:
                for j in range(UB):
                    body(k, B_LOOP + j)
            for c in range(B_END, QUADS + 1):
                body(0, c)

        def group(k, c):
            if isinstance(k, int) and not 0 <= c < GROUPS:
                return None
            return Step(UA, k, c)

        def quad(k, c):
            if isinstance(k, int) and not 0 <= c < QUADS:
                return None
            return Step(UB, k, c)

        def fill(eng, experts):
            eng.wait_ge(fill_ok, 1)
            for e in experts:
                r = eng.value_load(fill_row[0:1, e:e + 1], min_val=0, max_val=E * REGION - P)
                eng.dma_start(table[bass.ds(r, P)], filler[:]).then_inc(fill_in, 16)

        def table_written(eng):
            eng.wait_ge(fill_in, 16 * (1 + E))
            for s in range(UA):
                eng.wait_ge(scattered[s], 16 * T * len(range(s, GROUPS, UA)))

        def tile_start(eng, n, t):
            return eng.value_load(tile_row[t:t + 1, bass.ds(n, 1)], min_val=0, max_val=E * REGION)

        def expert_column(eng, q, t):
            return eng.value_load(tile_col[t:t + 1, bass.ds(q.n, 1)], min_val=0, max_val=(E - 1) * D)

        def load_tiles(eng, q, tiles):
            for t in tiles:
                r = tile_start(eng, q.n, t)
                eng.dma_start(rows_b[:, q.slot, t], table[bass.ds(r, P)]).then_inc(b_load[q.slot], 16)

        @block.sync
        def _(sp):
            def load_group(g):
                after(sp, x1_ok, g.n - UA + 1)
                sp.dma_start(x_in[:, g.slot], x_view[bass.ds(g.n, 1)].rearrange("a p t f -> (a p) t f")
                             ).then_inc(x_load[g.slot], 16)
                after(sp, at_ps, g.n - UA + 1)
                sp.dma_start(adj_in[:, g.slot], adj_view[bass.ds(g.n, 1)].rearrange("a p t f -> (a p) t f")
                             ).then_inc(a_load[g.slot], 16)

            load_group(Step(UA, 0, 0))
            load_group(Step(UA, 0, 1))
            sp.wait_ge(gnn_b_step, 5)
            for part in range(3):
                sp.dma_start(gnn_b3[part:part + 1], gnn_b_part[:, part].rearrange("a t f -> a (t f)")
                             ).then_inc(gnn_b_in, 16)

            def body(k, c):
                if g := group(k, c + 3):
                    load_group(g)
                if isinstance(k, int) and c == 1:
                    sp.dma_start(bd_all[:], bd.rearrange("(a e) c -> a (e c)", a=1).to_broadcast([P, E * D])
                                 ).then_inc(bd_in, 16)
                    for h in range(HC):
                        sp.dma_start(wd_sb[:, h].rearrange("p (e o) -> p e o", e=E),
                                     wd[:, h * P:(h + 1) * P].rearrange("e p o -> p e o")).then_inc(experts_in, 16)

            phase_a(sp, body)

            sp.dma_start(table[E * REGION:E * REGION + P], filler[:]).then_inc(fill_in, 16)
            fill(sp, range(E // 2))
            sp.wait_ge(tab_ok, 1)
            first = [tile_start(sp, 0, t) for t in range(T // 2)]
            table_written(sp)
            for t in range(T // 2):
                sp.dma_start(rows_b[:, 0, t], table[bass.ds(first[t], P)]).then_inc(b_load[0], 16)
            load_tiles(sp, Step(UB, 0, 1), range(T // 2))
            for n in range(2, UB):
                load_tiles(sp, Step(UB, 0, n), range(T))

            def body(k, c):
                q = quad(k, c + UB - 1)
                if q and not (q.fixed and q.n < UB):
                    sp.wait_ge(res_ok, T * (q.n - UB + 1))
                    load_tiles(sp, q, range(T))

            phase_b(sp, body)

        @block.gpsimd
        def _(pool):
            pool.memset(bg_col[:], 0.0).then_inc(const_pool, 1)
            pool.memset(minus_half[:], -0.5)
            pool.memset(bn[:], 0.0)
            pool.memset(pow_in[:], 1.0)
            pool.memset(group_tokens[:], float(GT))
            pool.memset(pace[:], 0.0)
            pool.memset(ident[:], 0.0)
            pool.memset(earlier[:], 1.0)
            pool.memset(ones[:], 1.0)
            pool.memset(wg_sb[:], 0.0)
            pool.memset(upto[:], 1.0)
            pool.memset(filler[:], 0.0)
            pool.iota(region_i[:], [[REGION // P, E]], base=0, channel_multiplier=0)
            pool.iota(tile_no_i[:], [[T, QUADS]], base=0, channel_multiplier=1)
            pool.iota(seed_tok[:], [[P, T]], base=0, channel_multiplier=1)
            pool.iota(first_wins[:], [[0, T], [-1, E]], base=E, channel_multiplier=0,
                      allow_small_or_imprecise_dtypes=True).then_inc(const_pool, 1)
            pool.wait_ge(const_pool, 2)
            pool.affine_select(out=ident[:], in_=ident[:], compare_op=ALU.not_equal, fill=1.0, base=0,
                               pattern=[[-1, P]], channel_multiplier=1)
            pool.affine_select(out=earlier[:], in_=earlier[:], compare_op=ALU.is_gt, fill=0.0, base=0,
                               pattern=[[1, P]], channel_multiplier=-1)
            pool.affine_select(out=upto[:], in_=upto[:], compare_op=ALU.is_ge, fill=0.0, base=0,
                               pattern=[[1, E], [-1, E]], channel_multiplier=0).then_inc(const_pool, 1)
            def powers1(g):
                pool.wait_ge(stat, g.n + 1)
                after(pool, xhat_act, g.n)
                after(pool, xhat_ok, g.n)
                pool.tensor_tensor(pow_out[:], pow_in[:, T:3 * T], minus_half[:], ALU.pow).then_inc(pow1, 1)

            def powers2(g):
                pool.wait_ge(stat, g.n + 3)
                pool.tensor_tensor(rows[:, g.slot, :, C_RSTD], pow_in[:, 0:T], minus_half[:, 0:T], ALU.pow
                                   ).then_inc(pow2, 1)

            def scatter(g):
                pool.wait_ge(row_ok, g.n + 1)
                after(pool, numbered, g.n)
                if not (g.fixed and g.n == GROUPS - 1):
                    pool.tensor_tensor(rows[:, (g.slot + 1) % UA, :, C_TOK], rows[:, g.slot, :, C_TOK],
                                       group_tokens[:], ALU.add).then_inc(numbered, 1)
                for t in range(T):
                    pool.indirect_dma_start(table, bass.IndirectOffsetOnAxis(ap=index[:, g.slot, t:t + 1], axis=0),
                                            rows[:, g.slot, t], None).then_inc(scattered[g.slot], 16)

            def body(k, c):
                if g := group(k, c + 1):
                    powers1(g)
                if g := group(k, c - 1):
                    powers2(g)
                if g := group(k, c - 4):
                    scatter(g)
                if isinstance(k, int) and c == 0:
                    pool.wait_ge(ffn_in, 16 * 4)
                    pool.tensor_copy(wg_sb[:, :, 0:E], wg_in[:]).then_inc(const_pool, 1)

            phase_a(pool, body)

            last_token = pool.to_reg(TOKENS - 1)

            def store(q):
                if not q.fixed:
                    pool.wait_ge(res_ok, T * (q.n + 1))
                after(pool, paced, q.n)
                pool.tensor_tensor(pace_out[:, q.slot:q.slot + 1], pace[:], pace[:], ALU.add).then_inc(paced, 1)
                for t in range(T):
                    if q.fixed:
                        pool.wait_ge(res_ok, T * q.n + t + 1)
                    pool.indirect_dma_start(
                        out_rows, bass.IndirectOffsetOnAxis(
                            ap=token[:, q.slot, t:t + 1], axis=0),
                        result[:, q.slot, t], None, bounds_check=last_token, oob_is_err=False,
                    ).then_inc(stored[q.slot], 16)

            def body(k, c):
                if q := quad(k, c - 1):
                    store(q)

            phase_b(pool, body)
            for s in range(UB):
                pool.wait_ge(stored[s], 16 * T * len(range(s, QUADS, UB)))

        @block.tensor
        def _(pe):
            pe.wait_ge(const_pool, 3)
            pe.wait_ge(gnn_in, 16 * 2)
            pe.transpose(ps_f[:, 0:P], gnn_w_sb[:], ident[:]).then_inc(wt_ps, 1)
            pe.wait_ge(wt_sb, 1)

            def xhat_transposes(g):
                pe.wait_ge(xhat_ok, g.n + 1)
                pe.wait_ge(xhat_act, g.n + 1)
                after(pe, at_sb, g.n)
                for t in range(T):
                    last = pe.transpose(ps_a[:, t * P:(t + 1) * P], xhat[:, t], ident[:])
                last.then_inc(xt_ps, 1)

            def adj_transposes(g):
                pe.wait_ge(a_load[g.slot], 16 * (g.nth + 1))
                pe.wait_ge(xt_sb, g.n + 1)
                for t in range(T):
                    last = pe.transpose(ps_a[:, t * P:(t + 1) * P], adj_in[:, g.slot, t], ident[:])
                last.then_inc(at_ps, 1)

            def features(g):
                pe.wait_ge(xt_sb, g.n + 1)
                if g.fixed and g.n == 0:
                    pe.wait_ge(gnn_b_in, 16 * 3)
                after(pe, f_sb, g.n)
                pe.matmul(ps_f[:], ones[0:3, :], gnn_b3[:], start=True, stop=False, skip_group_check=True)
                for t in range(T):
                    last = pe.matmul(ps_f[:, t * D:(t + 1) * D], xhat_t[:, t * P:(t + 1) * P], gnn_wt[:],
                                     start=False, stop=(t == T - 1), skip_group_check=True)
                last.then_inc(f_ps, 1)

            def aggregate(g):
                pe.wait_ge(f_sb, g.n + 1)
                pe.wait_ge(at_sb, g.n + 1)
                after(pe, agg_ok, g.n)
                for t in range(T):
                    last = pe.matmul(ps_u[:, t * D:(t + 1) * D], adj_t[:, t], feats[:, t], start=True, stop=True)
                last.then_inc(u_ps, 1)

            def x2_transposes(g):
                pe.wait_ge(x2hat_ok, g.n + 1)
                after(pe, x2lo_sb, g.n)
                for t in range(T):
                    last = pe.transpose(ps_x[:, t * P:(t + 1) * P], x2hat[:, t], ident[:])
                last.then_inc(x2t_ps, 1)

            def hidden_chunk(g, c):
                if c == 0:
                    pe.wait_ge(x2hi_sb, g.n + 1)
                    pe.wait_ge(x2lo_sb, g.n + 1)
                    if g.fixed and g.n == 0:
                        pe.wait_ge(const_dve, 2)
                after(pe, h_sb, HC * g.n + c - 1)
                w = slice(c * P, (c + 1) * P)
                pe.matmul(ps_h[c % 2][:], w1_hi[:, w], x2hat_hi[:, g.slot2], start=True, stop=False)
                pe.matmul(ps_h[c % 2][:], w1_hi[:, w], x2hat_lo[:, g.slot2], start=False, stop=False)
                pe.matmul(ps_h[c % 2][:], w1_lo[:, w], x2hat_hi[:, g.slot2], start=False, stop=True
                          ).then_inc(h_ps, 1)

            def gate(g):
                pe.wait_ge(h_sb, HC * (g.n + 1))
                if g.fixed and g.n == 0:
                    pe.wait_ge(const_pool, 4)
                after(pe, lt_sb, g.n)
                for c in range(HC):
                    last = pe.matmul(ps_g[32 * c:32 * c + 32], wg_sb[:, c], hidden[:, 0, c], start=True, stop=True)
                last.then_inc(g_ps, 1)

            def logits(g):
                pe.wait_ge(lt_sb, g.n + 1)
                after(pe, row_ok, g.n)
                for t in range(T):
                    last = pe.transpose(ps_r[:, t * P:(t + 1) * P], logits_t[:, t * P:(t + 1) * P], ident[:])
                last.then_inc(l_ps, 1)

            def ranks(g):
                pe.wait_ge(chosen_ok, g.n + 1)
                pe.matmul(rank_ps[:, 0:T], earlier[:], chosen[:], start=True, stop=False, skip_group_check=True)
                for t in range(T):
                    n = T - t
                    last = pe.matmul(rank_ps[:, t + 1:T + 1], ones[:],
                                     chosen[:, t:t + 1].to_broadcast([P, n, E]), start=False, stop=(t == T - 1),
                                     skip_group_check=True)
                last.then_inc(rank_ok, 1)

            def body(k, c):
                nxt, cur, two, three = (group(k, c + d) for d in (1, 0, -2, -3))
                if two:
                    x2_transposes(two)
                if cur:
                    adj_transposes(cur)
                if three:
                    gate(three)
                if cur:
                    features(cur)
                if two and not cur:
                    hidden_chunk(two, 0)
                if three:
                    logits(three)
                if two and cur:
                    hidden_chunk(two, 0)
                if two:
                    hidden_chunk(two, 1)
                if cur:
                    aggregate(cur)
                if two:
                    hidden_chunk(two, 2)
                if three:
                    ranks(three)
                if nxt:
                    xhat_transposes(nxt)
                if two:
                    hidden_chunk(two, 3)

            phase_a(pe, body)

            pe.wait_ge(experts_in, 16 * HC)
            pe.wait_ge(tab_ok, 1)

            def yhat_transposes(q):
                pe.wait_ge(yhat_ok, q.n + 1)
                after(pe, ylo_sb, q.n)
                for t in range(T):
                    last = pe.transpose(ps_x[:, t * P:(t + 1) * P], yhat[:, t], ident[:])
                last.then_inc(yt_ps, 1)

            def hidden_b(q, c):
                if c == 0:
                    pe.wait_ge(yhi_sb, q.n + 1)
                    pe.wait_ge(ylo_sb, q.n + 1)
                after(pe, bh_sb, HC * q.n + c - 1)
                w = slice(c * P, (c + 1) * P)
                pe.matmul(ps_h[c % 2][:], w1_hi[:, w], yhat_hi[:, q.slot2], start=True, stop=False)
                pe.matmul(ps_h[c % 2][:], w1_hi[:, w], yhat_lo[:, q.slot2], start=False, stop=False)
                pe.matmul(ps_h[c % 2][:], w1_lo[:, w], yhat_hi[:, q.slot2], start=False, stop=True
                          ).then_inc(bh_ps, 1)

            def expert(q, t, col):
                if t == 0:
                    pe.wait_ge(bh_sb, HC * (q.n + 1))
                after(pe, res_ok, T * (q.n - 1) + t + 1)
                for c in range(HC):
                    last = pe.matmul(ps_y[t][:, 0:D], hidden[:, q.slot2, c, t * P:(t + 1) * P],
                                     wd_sb[:, c, bass.ds(col, D)], start=(c == 0), stop=(c == HC - 1))
                last.then_inc(y_ps, 1)

            def body(k, c):
                prev, cur, nxt = quad(k, c - 1), quad(k, c), quad(k, c + 1)
                if cur:
                    hidden_b(cur, 0)
                if prev:
                    col0 = expert_column(pe, prev, 0)
                if nxt:
                    yhat_transposes(nxt)
                if cur:
                    hidden_b(cur, 1)
                if prev:
                    col1 = expert_column(pe, prev, 1)
                    expert(prev, 0, col0)
                    expert(prev, 1, col1)
                if cur:
                    hidden_b(cur, 2)
                if prev:
                    expert(prev, 2, expert_column(pe, prev, 2))
                if cur:
                    hidden_b(cur, 3)
                if prev:
                    expert(prev, 3, expert_column(pe, prev, 3))

            phase_b(pe, body)

        @block.scalar
        def _(act):
            act.dma_start(gnn_w_sb[:], gnn_w).then_inc(gnn_in, 16)
            act.dma_start(gnn_b_row[:], gnn_b.rearrange("(a f) -> a f", a=1)).then_inc(gnn_in, 16)
            act.dma_start(w1_sb[:], w1).then_inc(ffn_in, 16)
            act.dma_start(b1_col[:], b1.rearrange("(c p) -> p c", p=P), allow_slow_non_contiguous=True
                          ).then_inc(ffn_in, 16)
            act.dma_start(wg_in[:], wg.rearrange("(c p) e -> p c e", p=P)).then_inc(ffn_in, 16)
            act.wait_ge(const_pool, 1)
            act.dma_start(bg_col[0:E], bg.rearrange("(e a) -> e a", a=1)).then_inc(ffn_in, 16)

            act.wait_ge(const_pool, 2)
            act.activation(gelu_warm[:], pace[:], ACT.Gelu)

            def normalize1(g):
                act.wait_ge(shift1_ok, g.n + 1)
                after(act, xt_ps, g.n)
                for t in range(DVE_TILES, T):
                    last = act.activation(xhat[:, t], x_in[:, g.slot, t], ACT.Identity, bias=shift1[:, t:t + 1],
                                          scale=pow_out[:, t:t + 1])
                last.then_inc(xhat_act, 1)

            def xhat_copy(g):
                act.wait_ge(xt_ps, g.n + 1)
                after(act, f_ps, g.n)
                act.copy(xhat_t[:], ps_a[:]).then_inc(xt_sb, 1)

            def adj_copy(g):
                act.wait_ge(at_ps, g.n + 1)
                after(act, u_ps, g.n)
                act.copy(adj_t[:].rearrange("p t m -> p (t m)"), ps_a[:]).then_inc(at_sb, 1)

            def feats_copy(g):
                act.wait_ge(f_ps, g.n + 1)
                act.wait_ge(dinv_ok, g.n + 1)
                after(act, u_ps, g.n)
                for t in range(T):
                    last = act.activation(feats[:, t], ps_f[:, t * D:(t + 1) * D], ACT.Copy,
                                          scale=dinv[:, g.slot2, t:t + 1])
                last.then_inc(f_sb, 1)

            def relu(g):
                act.wait_ge(u_ps, g.n + 1)
                after(act, x1_ok, g.n)
                for t in range(T):
                    last = act.activation(agg[:, t], ps_u[:, t * D:(t + 1) * D], ACT.Relu,
                                          scale=dinv[:, g.slot2, t:t + 1])
                last.then_inc(agg_ok, 1)

            def x2_copy(g):
                act.wait_ge(x2t_ps, g.n + 1)
                after(act, h_ps, HC * (g.n - 1))
                act.copy(x2hat_hi[:, g.slot2], ps_x[:]).then_inc(x2hi_sb, 1)

            def gelu(g, c):
                act.wait_ge(h_ps, HC * g.n + c + 1)
                if g.fixed and g.n == 0 and c == 0:
                    act.wait_ge(ffn_in, 16 * 4)
                after(act, g_ps, g.n)
                act.activation(hidden[:, 0, c], ps_h[c % 2][:], ACT.Gelu, bias=b1_col[:, c:c + 1]).then_inc(h_sb, 1)

            def logits_copy(g):
                act.wait_ge(g_ps, g.n + 1)
                after(act, l_ps, g.n)
                act.activation(logits_t[:], ps_g[:], ACT.Identity, bias=bg_col[:, 0:1]).then_inc(lt_sb, 1)

            def body(k, c):
                nxt, cur, two, three = (group(k, c + d) for d in (1, 0, -2, -3))
                if two:
                    x2_copy(two)
                if cur:
                    adj_copy(cur)
                if three:
                    logits_copy(three)
                if cur:
                    feats_copy(cur)
                if two:
                    gelu(two, 0)
                if nxt:
                    normalize1(nxt)
                if two:
                    gelu(two, 1)
                if cur:
                    relu(cur)
                if two:
                    gelu(two, 2)
                if nxt:
                    xhat_copy(nxt)
                if two:
                    gelu(two, 3)

            phase_a(act, body)

            fill(act, range(E // 2, E))
            act.wait_ge(tab_ok, 1)
            first = [tile_start(act, 0, t) for t in range(T // 2, T)]
            table_written(act)
            for t in range(T // 2, T):
                act.dma_start(rows_b[:, 0, t], table[bass.ds(first[t - T // 2], P)]).then_inc(b_load[0], 16)
            load_tiles(act, Step(UB, 0, 1), range(T // 2, T))

            def yhat_copy(q):
                act.wait_ge(yt_ps, q.n + 1)
                after(act, bh_ps, HC * (q.n - 1))
                act.copy(yhat_hi[:, q.slot2], ps_x[:]).then_inc(yhi_sb, 1)

            def gelu_b(q, c):
                act.wait_ge(bh_ps, HC * q.n + c + 1)
                after(act, y_ps, T * (q.n - 1))
                act.activation(hidden[:, q.slot2, c], ps_h[c % 2][:], ACT.Gelu, bias=b1_col[:, c:c + 1]
                               ).then_inc(bh_sb, 1)

            def copy_bias(q, t):
                if t == 0:
                    after(act, biased_ok, q.n - 1)
                ins = act.copy(bias_copy[:, q.slot2, t], bd_all[:, bass.ds(expert_column(act, q, t), D)])
                if t == COPIED_BIASES - 1:
                    ins.then_inc(bias_ok, 1)

            def tanh(q):
                act.wait_ge(b_load[q.slot], 16 * T * (q.nth + 1))
                after(act, prob_ok, q.n)
                act.activation(tanh_half[:], rows_b[:, q.slot, :, C_BELOW:C_BELOW + E], ACT.Tanh, scale=0.5
                               ).then_inc(tanh_ok, 1)

            def body(k, c):
                cur, nxt = quad(k, c), quad(k, c + 1)
                if cur:
                    gelu_b(cur, 0)
                if nxt:
                    yhat_copy(nxt)
                if cur:
                    tanh(cur)
                    copy_bias(cur, 0)
                if cur:
                    gelu_b(cur, 1)
                    for t in range(1, COPIED_BIASES):
                        copy_bias(cur, t)
                    gelu_b(cur, 2)
                    gelu_b(cur, 3)

            act.wait_ge(bd_in, 16)
            phase_b(act, body)

        @block.vector
        def _(dve):
            dve.wait_ge(const_pool, 2)
            dve.tensor_copy(rows[:, 0, :, C_TOK], seed_tok[:])
            dve.tensor_copy(tile_no[:], tile_no_i[:])
            dve.tensor_scalar(base[:], region_i[:], float(P), None, ALU.mult)
            dve.tensor_scalar(region0[:], region_i[:], float(P), None, ALU.mult).then_inc(v1_setup, 1)
            dve.wait_ge(v1_setup, 1)
            dve.tensor_scalar(filler[:, C_TOK:C_TOK + 1], base[:, 0:1], 0.0, float(TOKENS),
                              ALU.mult, ALU.add).then_inc(v1_setup, 1)
            dve.wait_ge(wt_ps, 1)
            dve.tensor_copy(gnn_wt[:], ps_f[:, 0:P]).then_inc(wt_sb, 1)

            def split_gnn_b():
                dve.wait_ge(gnn_in, 16 * 2)
                rest = [gnn_b_row[:], gnn_b_rest[:, 0], gnn_b_rest[:, 1]]
                for part in range(3):
                    if part:
                        dve.wait_ge(gnn_b_step, 2 * part)
                    dve.tensor_copy(gnn_b_part[:, part], rest[part].rearrange("a (t f) -> a t f", t=1).to_broadcast(
                        [1, T, D])).then_inc(gnn_b_step, 1)
                    if part < 2:
                        dve.wait_ge(gnn_b_step, 2 * part + 1)
                        dve.tensor_tensor(rest[part + 1], rest[part], gnn_b_part[:, part, 0], ALU.subtract
                                          ).then_inc(gnn_b_step, 1)

            def split_w1():
                dve.wait_ge(ffn_in, 16 * 4)
                dve.tensor_copy(w1_hi[:], w1_sb[:]).then_inc(const_dve, 1)
                dve.wait_ge(const_dve, 1)
                dve.tensor_tensor(w1_lo[:], w1_sb[:], w1_hi[:].bitcast(F32), ALU.subtract).then_inc(const_dve, 1)

            def low2(g):
                dve.wait_ge(x2hi_sb, g.n + 1)
                after(dve, h_ps, HC * (g.n - 1))
                dve.tensor_tensor(x2hat_lo[:, g.slot2], ps_x[:], x2hat_hi[:, g.slot2].bitcast(F32), ALU.subtract
                                  ).then_inc(x2lo_sb, 1)

            def statistics(far, one, four, n):
                last = None

                def x1_tile(t):
                    if one:
                        return dve.bn_stats(bn[:, t], rows[:, one.slot, t, 0:D])

                if far:
                    dve.wait_ge(x_load[far.slot], 16 * (far.nth + 1))
                    for t in range(T):
                        last = dve.bn_stats(bn[:, T + t], x_in[:, far.slot, t])
                if one:
                    dve.wait_ge(agg_ok, one.n + 1)
                    after(dve, scattered[one.slot], 16 * T * one.nth)
                    dve.tensor_tensor(rows[:, one.slot, :, 0:D], agg[:], x_in[:, one.slot], ALU.add).then_inc(x1_ok, 1)
                if four:
                    dve.wait_ge(rank_ok, four.n + 1)
                    dve.tensor_tensor(place[:], rank_ps[:, 0:T], base[:].rearrange("p (a e) -> p a e", a=1
                                      ).to_broadcast([P, T, E]), ALU.add).then_inc(place_step, 1)
                if one:
                    dve.wait_ge(x1_ok, one.n + 1)
                x1_tile(0)
                if four:
                    dve.wait_ge(place_step, 2 * four.n + 1)
                    dve.tensor_tensor(place_own[:], place[:], chosen[:], ALU.mult).then_inc(place_step, 1)
                    dve.tensor_tensor(base[:], base[:], rank_ps[:, T], ALU.add)
                x1_tile(1)
                x1_tile(2)
                last = x1_tile(3) or last
                if last:
                    last.then_inc(moment_step, 1)
                if four:
                    dve.wait_ge(place_step, 2 * four.n + 2)
                    with nc.allow_low_precision("whole numbers below 2^24, seven of eight are zero"):
                        dve.tensor_reduce(index[:, four.slot], place_own[:], AX_X, ALU.add).then_inc(row_ok, 1)
                if far:
                    after(dve, pow1, far.n)
                    dve.wait_ge(deg_ok, far.n + 1)
                    dve.scalar_tensor_tensor(pow_in[:, 2 * T:3 * T], deg[:, far.slot2], 0.0, deg[:, far.slot2],
                                             ALU.is_equal, ALU.add)
                if not last:
                    return
                even, odd = bn[:, :, 0:3], bn[:, :, 3:6]
                dve.wait_ge(moment_step, 4 * n + 1)
                dve.tensor_tensor(m_sum[:], even[:, :, 1], odd[:, :, 1], ALU.add).then_inc(moment_step, 1)
                dve.tensor_tensor(m_diff[:], even[:, :, 1], odd[:, :, 1], ALU.subtract)
                dve.tensor_tensor(m_sq[:], even[:, :, 2], odd[:, :, 2], ALU.add).then_inc(moment_step, 1)
                dve.wait_ge(moment_step, 4 * n + 2)
                if far:
                    dve.tensor_scalar(mean1[:], m_sum[:, T:2 * T], 0.5, None, ALU.mult)
                if one:
                    dve.tensor_scalar(rows[:, one.slot, :, C_MEAN], m_sum[:, 0:T], 0.5, None, ALU.mult)
                    after(dve, pow2, one.n)
                dve.wait_ge(moment_step, 4 * n + 3)
                dve.scalar_tensor_tensor(m_between[:], m_diff[:], 0.25, m_diff[:], ALU.mult, ALU.mult)
                dve.tensor_scalar(m_within[:], m_sq[:], 1.0 / D, EPS, ALU.mult, ALU.add).then_inc(moment_step, 1)
                dve.wait_ge(moment_step, 4 * n + 4)
                dve.tensor_tensor(pow_in[:, 0:2 * T], m_within[:], m_between[:], ALU.add).then_inc(stat, 1)

            def normalize2(g, first, end):
                if first == 0:
                    dve.wait_ge(pow2, g.n + 1)
                    after(dve, x2t_ps, g.n)
                for t in range(first, end):
                    r = rows[:, g.slot, t]
                    last = dve.tensor_scalar(x2hat[:, t], r[:, 0:D], r[:, C_MEAN:C_MEAN + 1], r[:, C_RSTD:C_RSTD + 1],
                                             ALU.subtract, ALU.mult)
                if end == T:
                    last.then_inc(x2hat_ok, 1)

            def degrees(g):
                dve.wait_ge(a_load[g.slot], 16 * (g.nth + 1))
                after(dve, dinv_ok, g.n - 1)
                dve.tensor_reduce(deg[:, g.slot2], adj_in[:, g.slot], AX_X, ALU.add).then_inc(deg_ok, 1)

            def choose_and_normalize(three, nxt, one):
                def normalize_tile(t):
                    if nxt:
                        last = dve.tensor_scalar(xhat[:, t], x_in[:, nxt.slot, t], mean1[:, t:t + 1],
                                                 pow_out[:, t:t + 1], ALU.subtract, ALU.mult)
                        if t == DVE_TILES - 1:
                            last.then_inc(xhat_ok, 1)

                if three:
                    below = rows[:, three.slot, :, C_BELOW:C_BELOW + E]
                    dve.wait_ge(l_ps, three.n + 1)
                    dve.tensor_reduce(logit[:], partial_ps, AX_X, ALU.add).then_inc(choose_step, 1)
                    dve.wait_ge(choose_step, 5 * three.n + 1)
                    dve.tensor_reduce(top[:], logit[:], AX_X, ALU.max).then_inc(choose_step, 1)
                if nxt:
                    dve.wait_ge(pow1, nxt.n + 1)
                    after(dve, agg_ok, nxt.n - 1)
                    dve.scalar_tensor_tensor(dinv[:, nxt.slot2], deg[:, nxt.slot2], 0.0, pow_out[:, T:2 * T],
                                             ALU.not_equal, ALU.mult).then_inc(dinv_ok, 1)
                    after(dve, xhat_act, nxt.n)
                    dve.scalar_tensor_tensor(shift1[:], mean1[:], -1.0, pow_out[:, 0:T], ALU.mult, ALU.mult
                                             ).then_inc(shift1_ok, 1)
                    after(dve, xt_ps, nxt.n)
                if three:
                    dve.wait_ge(choose_step, 5 * three.n + 2)
                    dve.tensor_tensor(below, logit[:], top[:].rearrange("p (t a) -> p t a", a=1).to_broadcast(
                        [P, T, E]), ALU.subtract).then_inc(choose_step, 1)
                normalize_tile(0)
                if three:
                    dve.wait_ge(choose_step, 5 * three.n + 3)
                    dve.scalar_tensor_tensor(cand[:], below, 0.0, first_wins[:], ALU.is_equal, ALU.mult
                                             ).then_inc(choose_step, 1)
                normalize_tile(1)
                if three:
                    dve.wait_ge(choose_step, 5 * three.n + 4)
                    dve.tensor_reduce(best[:], cand[:], AX_X, ALU.max).then_inc(choose_step, 1)
                for t in range(2, DVE_TILES):
                    normalize_tile(t)
                if one:
                    normalize2(one, 0, 1)
                if three:
                    dve.wait_ge(choose_step, 5 * three.n + 5)
                    after(dve, place_step, 2 * three.n)
                    dve.tensor_tensor(chosen[:], cand[:], best[:].rearrange("p (t a) -> p t a", a=1).to_broadcast(
                        [P, T, E]), ALU.is_equal).then_inc(chosen_ok, 1)
                if one:
                    normalize2(one, 1, T)

            def body(k, c):
                far, nxt, one, two, three, four = (group(k, c + d) for d in (2, 1, -1, -2, -3, -4))
                if isinstance(k, int) and c == A_FIRST:
                    degrees(nxt)
                statistics(nxt, one, four, Step(UA, k, c + 1).n)
                if isinstance(k, int) and c == A_FIRST:
                    split_gnn_b()
                if two:
                    low2(two)
                if far:
                    degrees(far)
                choose_and_normalize(three, nxt, one)
                if isinstance(k, int) and c == 0:
                    split_w1()

            phase_a(dve, body)

            steps = [0]

            def link(ins):
                steps[0] += 1
                ins.then_inc(tab_step, 1)
                dve.wait_ge(tab_step, steps[0])

            dve.wait_ge(row_ok, GROUPS)
            dve.tensor_copy(fill_row[:], base[0:1, :]).then_inc(fill_ok, 1)
            link(dve.tensor_tensor(count_f[:], base[0:T, :], region0[0:T, :], ALU.subtract))
            link(dve.tensor_scalar(count_i[:], count_f[:], float(P - 1), None, ALU.add))
            link(dve.tensor_scalar(ntile_i[:], count_i[:], P.bit_length() - 1, None, ALU.logical_shift_right))
            link(dve.tensor_copy(ntile_f[:], ntile_i[:]))
            link(dve.tensor_tensor(ntile_upto[:], upto[:], ntile_f[:].rearrange("p (a e) -> p a e", a=1).to_broadcast(
                [T, E, E]), ALU.mult))
            link(dve.tensor_scalar(jump[:], ntile_f[:], -float(P), float(REGION), ALU.mult, ALU.add))
            link(dve.tensor_reduce(last_tile[:], ntile_upto[:], AX_X, ALU.add))
            link(dve.tensor_tensor(passed[:], tile_no[:].rearrange("p (j a) -> p j a", a=1).to_broadcast([T, QUADS, E]),
                                   last_tile[:].rearrange("p (a e) -> p a e", a=1).to_broadcast([T, QUADS, E]),
                                   ALU.is_ge))
            link(dve.tensor_tensor(jumped[:], passed[:], jump[:].rearrange("p (a e) -> p a e", a=1).to_broadcast(
                [T, QUADS, E]), ALU.mult))
            link(dve.tensor_reduce(tile_e[:], passed[:], AX_X, ALU.add))
            link(dve.tensor_reduce(tile_r[:], jumped[:], AX_X, ALU.add))
            link(dve.scalar_tensor_tensor(tile_r2[:], tile_no[:], float(P), tile_r[:], ALU.mult, ALU.add))
            link(dve.tensor_scalar(tile_row[:], tile_r2[:], float(E * REGION), None, ALU.min))
            link(dve.tensor_scalar(tile_col[:], tile_e[:], float(E - 1), float(D), ALU.min, ALU.mult))
            dve.engine_nop().then_inc(tab_ok, 1)

            def normalize_b(q):
                dve.wait_ge(b_load[q.slot], 16 * T * (q.nth + 1))
                after(dve, yt_ps, q.n)
                for t in range(T):
                    r = rows_b[:, q.slot, t]
                    last = dve.tensor_scalar(yhat[:, t], r[:, 0:D], r[:, C_MEAN:C_MEAN + 1], r[:, C_RSTD:C_RSTD + 1],
                                             ALU.subtract, ALU.mult)
                last.then_inc(yhat_ok, 1)

            def low_part(q):
                dve.wait_ge(yhi_sb, q.n + 1)
                dve.tensor_tensor(yhat_lo[:, q.slot2], ps_x[:], yhat_hi[:, q.slot2].bitcast(F32), ALU.subtract
                                  ).then_inc(ylo_sb, 1)

            def probability(q):
                dve.wait_ge(tanh_ok, q.n + 1)
                dve.tensor_scalar(soft[:], tanh_half[:], -1.0, 1.0, ALU.mult, ALU.add).then_inc(prob_step, 1)
                dve.wait_ge(prob_step, 4 * q.n + 1)
                dve.reciprocal(soft_r[:], soft[:]).then_inc(prob_step, 1)
                dve.wait_ge(prob_step, 4 * q.n + 2)
                dve.tensor_reduce(soft_sum[:], soft_r[:], AX_X, ALU.add).then_inc(prob_step, 1)
                dve.wait_ge(prob_step, 4 * q.n + 3)
                dve.tensor_scalar(denom[:], soft_sum[:], 2.0, -float(E), ALU.mult, ALU.add).then_inc(prob_step, 1)
                dve.wait_ge(prob_step, 4 * q.n + 4)
                dve.reciprocal(prob[:, q.slot2], denom[:]).then_inc(prob_ok, 1)

            def add_bias(q):
                dve.wait_ge(prob_ok, q.n + 1)
                after(dve, res_ok, T * (q.n - 1))
                for t in range(T):
                    if t < COPIED_BIASES:
                        if t == 0:
                            dve.wait_ge(bias_ok, q.n + 1)
                        bias = bias_copy[:, q.slot2, t]
                    else:
                        bias = bd_all[:, bass.ds(expert_column(dve, q, t), D)]
                    last = dve.scalar_tensor_tensor(biased[:, q.slot2, t], bias, prob[:, q.slot2, t:t + 1],
                                                    rows_b[:, q.slot, t, 0:D], ALU.mult, ALU.add)
                last.then_inc(biased_ok, 1)

            def results(q, t):
                dve.wait_ge(y_ps, T * q.n + t + 1)
                if t == 0:
                    dve.wait_ge(biased_ok, q.n + 1)
                    after(dve, stored[q.slot], 16 * T * q.nth)
                    dve.tensor_copy(token[:, q.slot], rows_b[:, q.slot, :, C_TOK])
                dve.scalar_tensor_tensor(result[:, q.slot, t], ps_y[t][:, 0:D], prob[:, q.slot2, t:t + 1],
                                         biased[:, q.slot2, t], ALU.mult, ALU.add).then_inc(res_ok, 1)

            def body(k, c):
                prev, cur, nxt, far = quad(k, c - 1), quad(k, c), quad(k, c + 1), quad(k, c + 2)
                if nxt and nxt.fixed and nxt.n == 0:
                    normalize_b(nxt)
                if nxt:
                    low_part(nxt)
                if prev:
                    results(prev, 0)
                    results(prev, 1)
                if far:
                    normalize_b(far)
                if prev:
                    results(prev, 2)
                    results(prev, 3)
                if cur:
                    probability(cur)
                    add_bias(cur)

            dve.wait_ge(bd_in, 16)
            phase_b(dve, body)


_INS = ["x", "adj", "L0_gnn_W", "L0_gnn_b", "L0_ffn_W1", "L0_ffn_b1", "L0_ffn_Wg", "L0_ffn_bg", "L0_ffn_Wd",
        "L0_ffn_bd"]


def kernel(**inputs):
    import numpy as _np
    import concourse.bacc as _bacc
    from concourse import mybir as _mybir
    from concourse.bass_utils import run_bass_kernel_spmd as _run

    nc = _bacc.Bacc("TRN2", target_bir_lowering=False, num_devices=1)
    arrays, args = {}, []
    for name in _INS:
        a = _np.ascontiguousarray(inputs[name])
        arrays[f"in_{name}_dram"] = a
        args.append(nc.dram_tensor(f"in_{name}_dram", a.shape, _mybir.dt.from_np(a.dtype), kind="ExternalInput").ap())
    result = nc.dram_tensor("out_0_dram", (GRAPHS, P, D), F32, kind="ExternalOutput").ap()
    moe_gnn_kernel(nc, *args, result)
    r = _run(nc, [arrays], core_ids=[0])
    return r.results[0]["out_0_dram"]
```
